# Optimizing a Trainium2 kernel written in Bass

```python
import numpy as np
import jax
import jax.numpy as jnp

def _softmax(x, axis=-1):
    return jax.nn.softmax(x, axis=axis)

def _gelu(x):
    return jax.nn.gelu(x, approximate=True)

def _silu(x):
    return jax.nn.silu(x)

def _sigmoid(x):
    return jax.nn.sigmoid(x)

def _layernorm(x, axis=-1, eps=1e-05):
    m = jnp.mean(x, axis=axis, keepdims=True)
    v = jnp.var(x, axis=axis, keepdims=True)
    return (x - m) / jnp.sqrt(v + eps)

def _scatter_add(tgt, idx, src, axis=0):
    return tgt.at[idx].add(src)

def _segment_sum(src, seg, n):
    return jax.ops.segment_sum(src, seg, n)
kernel_name = 'mk_adj_preln_d2_adj_r2_3d5ef0'

def setup_inputs(seed: int=0):
    np.random.seed(seed)
    _w = jnp.asarray

    def _rec_inputs():
        import jax
        import jax.numpy as jnp
        _gk = jax.random.key(seed)
        x = -0.0005963 + 1.001 * jax.random.normal(jax.random.fold_in(_gk, 1), (3327, 256), jnp.float32)
        _a = jax.random.bernoulli(jax.random.fold_in(_gk, 2), 0.00240457, (3327, 3327))
        _af = _a.astype(jnp.float32)
        adj = _af
        return (x, adj)
    x, adj = _rec_inputs()

    def _L0_gnn_setup():
        import jax, jax.numpy as jnp
        import numpy as np
        N = 3072
        D_IN = 256
        D_OUT = 256
        DENSITY = 0.005
        key = jax.random.key(seed)
        ks = jax.random.split(key, 12)
        x = jax.random.normal(ks[0], (N, D_IN), dtype=jnp.float32)
        adj_a = (jax.random.uniform(ks[1], (N, N)) < DENSITY).astype(jnp.float32)
        adj_b = (jax.random.uniform(ks[2], (N, N)) < DENSITY).astype(jnp.float32)
        W_sa = jax.random.normal(ks[3], (D_IN, D_OUT), dtype=jnp.float32) * (1.414 / np.sqrt(D_IN + D_OUT))
        a_sa = jax.random.normal(ks[4], (1, 2 * D_OUT), dtype=jnp.float32) * (1.414 / np.sqrt(1 + 2 * D_OUT))
        stdv = 1.0 / np.sqrt(D_OUT)
        W_gcnb = jax.random.uniform(ks[5], (D_IN, D_OUT), minval=-stdv, maxval=stdv, dtype=jnp.float32)
        b_gcnb = jax.random.uniform(ks[6], (D_OUT,), minval=-stdv, maxval=stdv, dtype=jnp.float32)
        s = 1.0 / np.sqrt(2 * D_IN)
        Wa = jax.random.uniform(ks[7], (1, 2 * D_IN), minval=-s, maxval=s, dtype=jnp.float32)
        ba = jax.random.uniform(ks[8], (1,), minval=-s, maxval=s, dtype=jnp.float32)
        Wb = jax.random.uniform(ks[9], (1, 2 * D_IN), minval=-s, maxval=s, dtype=jnp.float32)
        bb = jax.random.uniform(ks[10], (1,), minval=-s, maxval=s, dtype=jnp.float32)
        return {'x': x, 'adj_a': adj_a, 'adj_b': adj_b, 'W_sa': W_sa, 'a_sa': a_sa, 'W_gcnb': W_gcnb, 'b_gcnb': b_gcnb, 'Wa': Wa, 'ba': ba, 'Wb': Wb, 'bb': bb}
    _L0_gnn_all = _L0_gnn_setup()
    _L0_gnn_in = {k: v for k, v in _L0_gnn_all.items() if k in ('W_sa', 'a_sa', 'W_gcnb', 'b_gcnb', 'Wa', 'ba', 'Wb', 'bb')}
    del _L0_gnn_all

    def _L1_gnn_setup():
        import jax, jax.numpy as jnp
        import numpy as np
        N = 4096
        D = 256
        L = 2
        NEG_SLOPE = 0.01

        def _gat_layer(x, W, adj):
            proj = x @ W
            Wh, Ws = jnp.split(proj, 2, axis=-1)
            scores = Wh @ Ws.T
            a = jax.nn.softmax(scores, axis=-1) * adj
            out = a @ Wh
            out = out + x
            return jax.nn.leaky_relu(out, NEG_SLOPE)
        key = jax.random.key(seed)
        k1, k2, k3 = jax.random.split(key, 3)
        inputs = jax.random.normal(k1, (N, D), dtype=jnp.float32)
        adj = jax.random.randint(k2, (N, N), 0, 2).astype(jnp.float32)
        W_stack = jax.random.normal(k3, (L, D, 2 * D), dtype=jnp.float32) * (1.0 / np.sqrt(D))
        return {'inputs': inputs, 'adj': adj, 'W_stack': W_stack}
    _L1_gnn_all = _L1_gnn_setup()
    _L1_gnn_in = {k: v for k, v in _L1_gnn_all.items() if k in ('W_stack',)}
    del _L1_gnn_all
    return {'x': x, 'adj': adj, 'L0_gnn_W_sa': _L0_gnn_in['W_sa'], 'L0_gnn_a_sa': _L0_gnn_in['a_sa'], 'L0_gnn_W_gcnb': _L0_gnn_in['W_gcnb'], 'L0_gnn_b_gcnb': _L0_gnn_in['b_gcnb'], 'L0_gnn_Wa': _L0_gnn_in['Wa'], 'L0_gnn_ba': _L0_gnn_in['ba'], 'L0_gnn_Wb': _L0_gnn_in['Wb'], 'L0_gnn_bb': _L0_gnn_in['bb'], 'L1_gnn_W_stack': _L1_gnn_in['W_stack']}

def reference(x, adj, L0_gnn_W_sa, L0_gnn_a_sa, L0_gnn_W_gcnb, L0_gnn_b_gcnb, L0_gnn_Wa, L0_gnn_ba, L0_gnn_Wb, L0_gnn_bb, L1_gnn_W_stack):
    import jax
    import jax.numpy as jnp

    def _L0_gnn_ref(x, adj_a, adj_b, W_sa, a_sa, W_gcnb, b_gcnb, Wa, ba, Wb, bb):
        import jax, jax.numpy as jnp
        import numpy as np
        N = 3072
        D_IN = 256
        D_OUT = 256
        DENSITY = 0.005
        type_sum_a = adj_a @ x
        type_sum_b = adj_b @ x
        attn_a = jax.nn.sigmoid(jnp.concatenate([type_sum_a, x], axis=1) @ Wa.T + ba)
        attn_b = jax.nn.sigmoid(jnp.concatenate([type_sum_b, x], axis=1) @ Wb.T + bb)
        h = x @ W_sa
        Hd = h.shape[1]
        s_left = h @ a_sa[0, :Hd]
        s_right = h @ a_sa[0, Hd:]
        scores = s_left[:, None] + s_right[None, :]
        e = jnp.where(adj_a != 0, jnp.exp(-jax.nn.leaky_relu(scores, 0.01)), 0.0)
        attn = e / (jnp.sum(e, axis=1, keepdims=True) + 1e-05)
        x_a = attn @ h
        x_b = adj_b @ (x @ W_gcnb) + b_gcnb
        return jax.nn.sigmoid(attn_a * x_a + attn_b * x_b)

    def _L1_gnn_ref(inputs, adj, W_stack):
        import jax, jax.numpy as jnp
        import numpy as np
        N = 4096
        D = 256
        L = 2
        NEG_SLOPE = 0.01

        def _gat_layer(x, W, adj):
            proj = x @ W
            Wh, Ws = jnp.split(proj, 2, axis=-1)
            scores = Wh @ Ws.T
            a = jax.nn.softmax(scores, axis=-1) * adj
            out = a @ Wh
            out = out + x
            return jax.nn.leaky_relu(out, NEG_SLOPE)
        x = inputs
        for l in range(W_stack.shape[0]):
            x = _gat_layer(x, W_stack[l], adj)
        return x
    h = jnp.maximum(_layernorm(x, axis=-1), 0.0)
    x = x + _L0_gnn_ref(h, adj, adj, L0_gnn_W_sa, L0_gnn_a_sa, L0_gnn_W_gcnb, L0_gnn_b_gcnb, L0_gnn_Wa, L0_gnn_ba, L0_gnn_Wb, L0_gnn_bb)
    h = jnp.maximum(_layernorm(x, axis=-1), 0.0)
    x = x + _L1_gnn_ref(h, adj, L1_gnn_W_stack)
    return x

_drawn_inputs = setup_inputs


def setup_inputs(seed=0):
    import zlib

    import numpy as np

    out = dict(_drawn_inputs(seed))
    spreads = {}
    factors = {'L0_gnn_a_sa': 8.0, 'L0_gnn_b_gcnb': 8.0, 'L0_gnn_Wa': 4.345, 'L1_gnn_W_stack': 3.669}
    for name, (base, spread) in spreads.items():
        noise = np.random.default_rng([zlib.crc32(name.encode()), seed]).standard_normal(out[name].shape)
        drawn = base * np.exp(spread * noise) if base else spread * noise
        out[name] = jnp.asarray(drawn.astype(out[name].dtype))
    for name, factor in factors.items():
        out[name] = (out[name] * factor).astype(out[name].dtype)
    return out
```

```python
from contextlib import ExitStack

import concourse.bass as bass
from concourse import mybir

F32 = mybir.dt.float32
F32R = mybir.dt.float32r
U8 = mybir.dt.uint8
ALU = mybir.AluOpType
ACT = mybir.ActivationFunctionType
AX = mybir.AxisListType.X

P = 128
N = 3327
T = (N + P - 1) // P
NP = T * P
D = 256
K = D // P
PAIRS = T // 2
LAYERS = 2
SLOPE = 0.01
EPS_LN = 1e-5
EPS_DEN = 1e-5

GX = D + 2
HX = D + 4
WC = GX + HX + 2

UNITS = T // 2
PART_J = [(0, 16), (16, T)]
C = 512
CHUNKS = (N + C - 1) // C
WIDTH = [C] * (CHUNKS - 1) + [NP - C * (CHUNKS - 1)]
REAL = [C] * (CHUNKS - 1) + [N - C * (CHUNKS - 1)]
BODY = 2 * CHUNKS

LEAD = 14


def ring(slots, last=()):
    def build(steps):
        whole = (steps - len(last)) if last else steps
        return [i % slots for i in range(whole)] + list(last)
    return build


def before(slots, i):
    n = len(slots)
    j = i - 1
    while slots[j % n] != slots[i]:
        j -= 1
    return j


STAGE = ring(6, [3])(UNITS)
WORK1 = ring(5)(UNITS)
HALF1 = ring(3, [1])(UNITS)
SBANK = ring(5)(BODY)
TBANK = ring(2)(BODY)
WORK2 = ring(5)(BODY)
HALF2 = ring(3)(BODY)


def two_graph_blocks(nc, xt, adjt, wx, rows, wst, out):
    ctx = ExitStack()
    with ctx:
        def sb(name, shape, dt):
            return ctx.enter_context(nc.sbuf_tensor(name, shape, dt))

        def sem(name):
            return ctx.enter_context(nc.semaphore(name))

        adj8_d = nc.dram_tensor("adj8_scratch", [PAIRS, P, T, 2 * P], U8).ap()
        whT_d = nc.dram_tensor("whT_scratch", [T, P, 2 * K * P], F32).ap()
        x1_d = nc.dram_tensor("x1_scratch", [T, P, D], F32).ap()

        X = sb("X", [P, T, D], F32)
        RA = sb("RA", [P, T, 516], F32R)
        RB = sb("RB", [P, T * 516], F32R)
        G = RB[:, :].rearrange("p (t c) -> p t c", t=T)
        WsT = RB[:, 0:2 * K * NP].rearrange("p (s k n) -> p s k n", s=2, k=K)
        ROW = sb("ROW", [P, 2, NP], F32)
        SLB = ROW[:, 0, :]
        STG = ROW[:, 1, 0:6 * C].rearrange("p (s c) -> p s c", s=6)
        WRAW0 = ROW[:, 1, 0:2 * WC].rearrange("p (k c) -> p k c", k=K)
        AROW = ROW[:, 1, 2 * WC:2 * WC + 2 * D]
        WRAW1 = ROW[:, 0, 0:K * 2 * D].rearrange("p (k c) -> p k c", k=K)
        AF = sb("AF", [P, 5, C], F32)
        HN = AF[:, 0, :].rearrange("p (h c) -> p h c", h=2)
        FR = sb("FR", [P, 9, C], F32R)
        AH, AL, RR = 0, 3, 6
        HT = [FR[:, 2 * b:2 * b + 2, :].rearrange("p s (k n) -> p s k n", k=K) for b in range(2)]
        WHS = FR[:, 4:6, :].rearrange("p h (s d n) -> p h s d n", s=2, d=K)
        WSL = FR[:, 8, :].rearrange("p (s k c) -> p s k c", s=2, k=K)
        A8 = sb("A8", [P, T, 2 * P], U8)
        WX = sb("WX", [P, 2, K, WC], F32R)
        PEB = sb("PEB", [P, 2, GX], F32)
        PAB = sb("PAB", [P, 2, GX], F32)
        BIAS = sb("BIAS", [P, GX], F32)
        IDN = sb("IDN", [P, P], F32)
        MV = sb("MV", [P, T, 2], F32)
        BN = sb("BN", [P, 2, 6], F32)
        LNT = sb("LNT", [P, 6, T], F32)
        RSTD, NMR = LNT[:, 4, :], LNT[:, 5, :]
        XA = sb("XA", [P, T, 2], F32)
        SR = sb("SR", [P, T], F32)
        COL = sb("COL", [P, 48], F32)
        WV = COL[:, 0:4].rearrange("p (s k) -> p s k", s=2)
        ZZ = COL[:, 4:8].rearrange("p (h c) -> p h c", h=2)
        SG = COL[:, 8:12].rearrange("p (h c) -> p h c", h=2)
        DN = COL[:, 12:14]
        CA = COL[:, 14:16]
        MX = COL[:, 16:16 + CHUNKS]
        SM = COL[:, 24:40].rearrange("p (h c) -> p h c", h=2)
        NMX = COL[:, 40:42]
        DEN = COL[:, 42:43]
        RIN = COL[:, 43:44]
        AG = COL[:, 44:48].rearrange("p (h c) -> p h c", h=2)
        PS = ctx.enter_context(nc.psum_tensor("PS", [P, 8, C], F32))

        x_in = [sem(f"x_in{i}") for i in range(2)]
        w_in = sem("w_in")
        const_in = sem("const_in")
        ident0 = sem("ident0")
        ident = sem("ident")
        stat = sem("stat")
        stat2 = sem("stat2")
        stat3 = sem("stat3")
        wv_step = sem("wv_step")
        w_ready = sem("w_ready")
        ln_in = sem("ln_in")
        ln_sqrt = sem("ln_sqrt")
        ln_step = sem("ln_step")
        ln_done = sem("ln_done")
        ones_set = sem("ones_set")

        hn_done = sem("hn_done")
        tp_done = sem("tp_done")
        hthi_done = sem("hthi_done")
        htlo_done = sem("htlo_done")
        sl_mm = sem("sl_mm")
        g_mm = sem("g_mm")
        h2_mm = sem("h2_mm")
        slb_done = sem("slb_done")
        ghi_done = sem("ghi_done")
        glo_done = sem("glo_done")
        h2hi_done = sem("h2hi_done")
        h2lo_done = sem("h2lo_done")

        stage_full = [sem(f"stage_full{i}") for i in range(6)]
        s_done = sem("s_done")
        bytes_out = [sem(f"bytes_out{i}") for i in range(6)]
        lr_done = sem("lr_done")
        e_done = sem("e_done")
        masked = sem("masked")
        adjr_done = sem("adjr_done")
        hi_done = sem("hi_done")
        lo_done = sem("lo_done")
        mm_done = sem("mm_done")
        first_done = sem("first_done")
        e_copied = sem("e_copied")
        a_copied = sem("a_copied")
        post1 = sem("post1")
        z_ready = sem("z_ready")
        sg_ready = sem("sg_ready")
        v_ready = sem("v_ready")
        th_ready = sem("th_ready")
        x1_ready = sem("x1_ready")
        x1_stored = sem("x1_stored")

        x_ready = sem("x_ready")
        w1_in = sem("w1_in")
        w1_hi = sem("w1_hi")
        w1_ready = sem("w1_ready")
        hn1_done = sem("hn1_done")
        tp1_done = sem("tp1_done")
        hthi1_done = sem("hthi1_done")
        htlo1_done = sem("htlo1_done")
        ws_mm = sem("ws_mm")
        wt_mm = sem("wt_mm")
        wh_mm = sem("wh_mm")
        wshi_done = sem("wshi_done")
        wslo_done = sem("wslo_done")
        wthi_done = sem("wthi_done")
        wtlo_done = sem("wtlo_done")
        whhi_done = sem("whhi_done")
        whlo_done = sem("whlo_done")
        whT_stored = sem("whT_stored")

        whT_full = [sem(f"whT_full{i}") for i in range(2)]
        adj8_full = [sem(f"adj8_full{i}") for i in range(2)]
        pad_zero = sem("pad_zero")
        sc_done = sem("sc_done")
        ev_done = sem("ev_done")
        max_done = sem("max_done")
        p_done = sem("p_done")
        t_done = sem("t_done")
        m_done = sem("m_done")
        ahi_done = sem("ahi_done")
        alo_done = sem("alo_done")
        av_done = sem("av_done")
        sum_step = sem("sum_step")
        rin_done = sem("rin_done")
        right_done = sem("right_done")
        o_read = sem("o_read")
        res_done = sem("res_done")

        x1_back = [sem(f"x1_back{i}") for i in range(2)]
        out_ready = sem("out_ready")
        out_stored = sem("out_stored")

        block = ctx.enter_context(nc.Block())

        stage_uses = [STAGE.count(s) for s in range(6)]

        def staged(pr, u):
            return pr * (16 * stage_uses[STAGE[u]]) + 16 * (STAGE[:u].count(STAGE[u]) + 1)


        @block.sync
        def _(sp):
            sp.sem_inc(whT_stored, 16)
            sp.dma_start(BIAS[:, :], rows[:, 2 * D:2 * D + GX]).then_inc(const_in, 16)
            sp.dma_start(AROW, rows[:, 0:2 * D]).then_inc(w_in, 16)
            sp.dma_start(WRAW0[:, :, 0:GX + D + 2], wx).then_inc(w_in, 16)
            half = 14
            sp.dma_start(X[:, 0:half, :], xt[:, 0:half, :]).then_inc(x_in[0], 16)
            sp.dma_start(X[:, half:T, :], xt[:, half:T, :]).then_inc(x_in[1], 16)

            sp.wait_ge(w_ready, 2)
            def load_unit(pr, u, first):
                b, n = before(STAGE, u), STAGE[:u].count(STAGE[u])
                if not (first and n == 0):
                    read = sp.to_reg(pr * UNITS + (LEAD + b + 1))
                    stored = sp.to_reg(pr * (16 * stage_uses[STAGE[u]]) + 16 * n)
                    sp.wait_ge(w_ready, 2)
                    sp.wait_ge(adjr_done, read)
                    sp.wait_ge(masked, read)
                    sp.wait_ge(bytes_out[STAGE[u]], stored)
                sp.dma_start(STG[:, STAGE[u], :],
                             adjt[bass.ds(pr, 1), :, 2 * u:2 * u + 2, :].rearrange("o p j i -> p (o j i)"))\
                    .then_inc(stage_full[STAGE[u]], 16)

            for u in range(UNITS):
                load_unit(0, u, True)
            with sp.Fori(1, PAIRS) as pr:
                for u in range(UNITS):
                    load_unit(pr, u, False)

            sp.wait_ge(s_done, PAIRS * UNITS)
            for i in range(6):
                sp.wait_ge(bytes_out[i], 16 * PAIRS * stage_uses[i])
            with sp.Fori(0, LAYERS) as layer:
                reached = sp.to_reg(layer * (PAIRS * BODY) + (LEAD - CHUNKS))
                sp.wait_ge(w_ready, 2)
                sp.wait_ge(t_done, reached)
                sp.dma_start(WRAW1, wst[bass.ds(layer, 1), :, :, :].rearrange("o p k c -> p (o k) c"))\
                  .then_inc(w1_in, 16)
                with sp.Fori(0, PAIRS) as pr:
                    reached = sp.to_reg(layer * PAIRS + pr + (1 + LEAD))
                    sp.wait_ge(w_ready, 2)
                    sp.wait_ge(wtlo_done, reached)
                    sp.dma_start(whT_d[bass.ds(2 * pr, 2), :, :].rearrange("t p f -> p t f"),
                                 FR[:, 4:6, :].bitcast(F32)).then_inc(whT_stored, 16)
                reached = sp.to_reg(layer * (16 * PAIRS) + (16 * PAIRS + 16))
                sp.wait_ge(w_ready, 2)
                sp.wait_ge(whT_stored, reached)
                with sp.Fori(0, PAIRS) as pr:
                    for h in range(2):
                        reached = sp.to_reg(layer * (PAIRS * BODY) + pr * BODY + (LEAD + CHUNKS * (h - 1)))
                        sp.wait_ge(w_ready, 2)
                        sp.wait_ge(sc_done, reached)
                        sp.dma_start(FR[:, RR + h, :].bitcast(F32),
                                     whT_d[bass.ds(2 * pr + h, 1), :, :].rearrange("o p f -> p (o f)"))\
                          .then_inc(whT_full[h], 16)
                    for g, (j0, j1) in enumerate(PART_J):
                        reached = sp.to_reg(layer * (PAIRS * BODY) + pr * BODY
                                            + (LEAD - CHUNKS + (j1 * P + C - 1) // C))
                        sp.wait_ge(w_ready, 2)
                        sp.wait_ge(m_done, reached)
                        sp.dma_start(A8[:, j0:j1, :],
                                     adj8_d[bass.ds(pr, 1), :, j0:j1, :].rearrange("o p j i -> p (o j) i"))\
                          .then_inc(adj8_full[g], 16)

            sp.wait_ge(t_done, LEAD + LAYERS * PAIRS * BODY)
            back = ROW[:, :, :].rearrange("p h (t d) -> p (h t) d", d=D)
            for i, (t0, t1) in enumerate(((0, PAIRS), (PAIRS, T))):
                sp.dma_start(back[:, t0:t1, :], x1_d[t0:t1, :, :].rearrange("t p d -> p t d"))\
                  .then_inc(x1_back[i], 16)
            full = T - 1
            sp.wait_ge(out_ready, 1)
            sp.dma_start(out[0:PAIRS * P, :].rearrange("(t p) d -> p t d", p=P), X[:, 0:PAIRS, :])\
              .then_inc(out_stored, 16)
            sp.wait_ge(out_ready, 2)
            sp.dma_start(out[PAIRS * P:full * P, :].rearrange("(t p) d -> p t d", p=P), X[:, PAIRS:full, :])\
              .then_inc(out_stored, 16)
            sp.dma_start(out[full * P:N, :], X[0:N - full * P, full, :]).then_inc(out_stored, 16)
            sp.wait_ge(out_stored, 48)
            sp.wait_ge(x1_stored, 16 * PAIRS)

        @block.gpsimd
        def _(pool):
            pool.sem_inc(alo_done, LEAD)
            nc.gpsimd.memset(IDN[:, :], 0.0).then_inc(ident0, 1)
            nc.gpsimd.memset(RA[:, :, D:D + 1].bitcast(F32), 1.0).then_inc(ones_set, 1)
            nc.gpsimd.memset(RA[:, :, D + 1:D + 2].bitcast(F32), 0.0).then_inc(ones_set, 1)
            pool.wait_ge(ident0, 1)
            nc.gpsimd.affine_select(out=IDN[:, :], in_=IDN[:, :], compare_op=ALU.not_equal, fill=1.0,
                                    base=0, pattern=[[-1, P]], channel_multiplier=1).then_inc(ident, 1)

            pool.wait_ge(slb_done, PAIRS + LEAD)
            pool.wait_ge(h2lo_done, T + LEAD)
            pool.wait_ge(htlo_done, PAIRS)
            with pool.Fori(0, PAIRS) as pr:
                for u in range(UNITS):
                    s = WORK1[u]
                    reached = pool.to_reg(pr * UNITS + (LEAD + before(WORK1, u) + 1))
                    pool.wait_ge(ident, 1)
                    pool.wait_ge(lo_done, reached)
                    nc.gpsimd.tensor_tensor(
                        AF[:, s, :].rearrange("p (j i) -> p j i", j=2),
                        SLB[:, bass.ds(pr * 256, 256)].unsqueeze(1).broadcast_to([P, 2, 256]),
                        SR[:, 2 * u:2 * u + 2].unsqueeze(2).broadcast_to([P, 2, 256]),
                        ALU.add).then_inc(s_done, 1)
                    landed = pool.to_reg(staged(pr, u))
                    pool.wait_ge(ident, 1)
                    pool.wait_ge(stage_full[STAGE[u]], landed)
                    pool.wait_ge(ident, 1)
                    pool.dma_start(adj8_d[bass.ds(pr, 1), :, 2 * u:2 * u + 2, :].rearrange("o p j i -> p (o j i)"),
                                   STG[:, STAGE[u], :]).then_inc(bytes_out[STAGE[u]], 16)

            with pool.Fori(0, LAYERS) as layer:
                with pool.Fori(0, PAIRS) as pr:
                    pool.wait_ge(x_ready, layer * T + pr * 2 + 2)
                    pool.wait_ge(tp1_done, layer * PAIRS + pr + LEAD)
                    reached = pool.to_reg(layer * (PAIRS * BODY) + LEAD)
                    pool.wait_ge(ident, 1)
                    pool.wait_ge(av_done, reached)
                    nc.gpsimd.tensor_copy(HN, X[:, bass.ds(2 * pr, 2), :]).then_inc(hn1_done, 1)
                with pool.Fori(0, PAIRS) as pr:
                    for c in range(BODY):
                        w = WIDTH[c % CHUNKS]
                        pool.wait_ge(ahi_done, layer * (PAIRS * BODY) + pr * BODY + (c + 1))
                        nc.gpsimd.tensor_tensor(FR[:, AL + HALF2[c], 0:w], AF[:, WORK2[c], 0:w],
                                                FR[:, AH + HALF2[c], 0:w].bitcast(F32), ALU.subtract)\
                          .then_inc(alo_done, 1)

        @block.scalar
        def _(act):
            for s in (slb_done, adjr_done, e_copied):
                act.sem_inc(s, LEAD)

            act.wait_ge(ln_in, 1)
            nc.scalar.activation(LNT[:, 1, :], LNT[:, 0, :], ACT.Sqrt).then_inc(ln_sqrt, 1)

            def normalise(pr):
                act.wait_ge(tp_done, pr + LEAD)
                for h in range(2):
                    last = nc.scalar.activation(HN[:, h, :], X[:, bass.ds(2 * pr + h, 1), :].squeeze(1),
                                                ACT.Relu, scale=RSTD[:, bass.ds(2 * pr + h, 1)],
                                                bias=NMR[:, bass.ds(2 * pr + h, 1)])
                last.then_inc(hn_done, 1)

            def transposed_high(pr, b):
                act.wait_ge(tp_done, pr + 1 + LEAD)
                if not isinstance(pr, int):
                    act.wait_ge(h2_mm, pr * 2 - 2 + LEAD)
                nc.scalar.activation(HT[b][:, 0, :, :], PS[:, 4, :].rearrange("p (k n) -> p k n", k=K),
                                     ACT.Copy).then_inc(hthi_done, 1)

            def outputs_high(pr):
                act.wait_ge(sl_mm, pr + 1)
                nc.scalar.activation(SLB[:, bass.ds(pr * 256, 256)], PS[:, 5, 0:256], ACT.Copy)\
                  .then_inc(slb_done, 1)
                for h in range(2):
                    act.wait_ge(g_mm, pr * 2 + (h + 1))
                    nc.scalar.activation(G[:, bass.ds(2 * pr + h, 1), 0:GX].squeeze(1),
                                         PS[:, h, 0:GX], ACT.Copy).then_inc(ghi_done, 1)
                for h in range(2):
                    act.wait_ge(h2_mm, pr * 2 + (h + 1) + LEAD)
                    nc.scalar.activation(RA[:, bass.ds(2 * pr + h, 1), 0:D].squeeze(1),
                                         PS[:, 2 + h, 0:D], ACT.Copy).then_inc(h2hi_done, 1)

            act.wait_ge(ln_done, 1)
            normalise(0)
            transposed_high(0, 0)
            with act.Fori(0, (PAIRS - 1) // 2) as half:
                p2 = half * 2
                for j in range(2):
                    normalise(p2 + (j + 1))
                    transposed_high(p2 + (j + 1), (j + 1) % 2)
                    outputs_high(p2 + j)
            outputs_high(PAIRS - 1)

            def exp1(pr, u):
                q, i = u // UNITS, u % UNITS
                s = AF[:, WORK1[i], :]
                act.wait_ge(lr_done, pr * UNITS + (u + 1))
                nc.scalar.activation(s, s, ACT.Exp, scale=-1.0).then_inc(e_done, 1)

            def high1(pr, u):
                q, i = u // UNITS, u % UNITS
                free = LEAD + q * UNITS + before(HALF1, i) + 1
                act.wait_ge(mm_done, pr * UNITS + free)
                act.wait_ge(stage_full[STAGE[i]], staged(pr + q, i))
                nc.scalar.activation(FR[:, RR + HALF1[i], :], STG[:, STAGE[i], :], ACT.Copy)\
                  .then_inc(adjr_done, 1)
                act.wait_ge(masked, pr * UNITS + (LEAD + u + 1))
                nc.scalar.activation(FR[:, AH + HALF1[i], :], AF[:, WORK1[i], :], ACT.Copy).then_inc(hi_done, 1)

            def post_copy(pr):
                for h in range(2):
                    if h == 0:
                        act.wait_ge(first_done, pr + 1)
                    else:
                        act.wait_ge(mm_done, pr * UNITS + (LEAD + UNITS))
                    nc.scalar.activation(PEB[:, h, :], PS[:, h, 0:GX], ACT.Copy).then_inc(e_copied, 1)

            def post_gates(pr):
                act.wait_ge(z_ready, pr + 1)
                nc.scalar.activation(SG, ZZ, ACT.Tanh, scale=0.5).then_inc(sg_ready, 1)

            def post_sigmoid(pr):
                act.wait_ge(v_ready, pr + 1)
                nc.scalar.activation(PEB[:, :, 0:D], PEB[:, :, 0:D], ACT.Tanh, scale=0.5).then_inc(th_ready, 1)

            def post_store(pr):
                act.wait_ge(x1_ready, pr + 1)
                act.dma_start(x1_d[bass.ds(2 * pr, 2), :, :].rearrange("t p d -> p t d"),
                              X[:, bass.ds(2 * pr, 2), :]).then_inc(x1_stored, 16)

            def units_act(pr, post, more):
                for u in range(UNITS):
                    if u + 2 < UNITS or more:
                        exp1(pr, u + 2)
                    if u + 1 < UNITS or more:
                        high1(pr, u + 1)
                    if post and u == 0:
                        post_copy(pr - 1)
                    if post and u == 1:
                        post_gates(pr - 1)
                    if post and u == 3:
                        post_sigmoid(pr - 1)
                    if post and u == 6:
                        post_store(pr - 1)

            exp1(0, 0)
            exp1(0, 1)
            high1(0, 0)
            units_act(0, False, True)
            with act.Fori(1, PAIRS - 1) as pr:
                units_act(pr, True, True)
            units_act(PAIRS - 1, True, False)
            post_copy(PAIRS - 1)
            post_gates(PAIRS - 1)
            post_sigmoid(PAIRS - 1)
            post_store(PAIRS - 1)

            act.wait_ge(ln_in, 2)
            nc.scalar.activation(LNT[:, 1, :], LNT[:, 0, :], ACT.Sqrt).then_inc(ln_sqrt, 1)
            act.wait_ge(ln_done, 2)
            act.wait_ge(x1_stored, 16 * PAIRS)
            with act.Fori(0, PAIRS) as pr:
                for h in range(2):
                    x = X[:, bass.ds(2 * pr + h, 1), :].squeeze(1)
                    nc.scalar.activation(x, x, ACT.Relu, scale=RSTD[:, bass.ds(2 * pr + h, 1)],
                                         bias=NMR[:, bass.ds(2 * pr + h, 1)]).then_inc(x_ready, 1)

            def transposed_high2(base, pr, b):
                act.wait_ge(tp1_done, base + (pr + 1) + LEAD)
                if not isinstance(pr, int):
                    act.wait_ge(wh_mm, base + (pr - 1) + LEAD)
                nc.scalar.activation(HT[b][:, 0, :, :], PS[:, 7, :].rearrange("p (k n) -> p k n", k=K),
                                     ACT.Copy).then_inc(hthi1_done, 1)

            def outputs_high2(base, pr):
                act.wait_ge(ws_mm, base + (pr + 1))
                nc.scalar.activation(WsT[:, 0, :, bass.ds(pr * 256, 256)],
                                     PS[:, 0, :].rearrange("p (k n) -> p k n", k=K), ACT.Copy)\
                  .then_inc(wshi_done, 1)
                act.wait_ge(wt_mm, base + (pr + 1))
                act.wait_ge(whT_stored, (base + pr) * 16 + 16)
                nc.scalar.activation(WHS[:, :, 0, :, :],
                                     PS[:, 1, :].rearrange("p (d h n) -> p h d n", d=K, h=2), ACT.Copy)\
                  .then_inc(wthi_done, 1)
                act.wait_ge(wh_mm, base + (pr + 1) + LEAD)
                nc.scalar.activation(RA[:, bass.ds(2 * pr, 2), 0:D],
                                     PS[:, 2, :].rearrange("p (h c) -> p h c", h=2), ACT.Copy)\
                  .then_inc(whhi_done, 1)

            def exps(tile, h):
                act.wait_ge(max_done, tile + 1)
                for c in range(CHUNKS):
                    r = ROW[:, h, c * C:c * C + REAL[c]]
                    nc.scalar.activation(r, r, ACT.Exp, bias=NMX[:, h:h + 1], accum_out=SM[:, h, c:c + 1])\
                      .then_inc(p_done, 1)

            def high2(chunks, c):
                w, s = WIDTH[c % CHUNKS], HALF2[c]
                act.wait_ge(m_done, chunks + (LEAD + c + 1))
                act.wait_ge(av_done, chunks + (LEAD + before(HALF2, c) + 1))
                nc.scalar.activation(FR[:, AH + s, 0:w], AF[:, WORK2[c], 0:w], ACT.Copy).then_inc(ahi_done, 1)

            def steps_act(chunks, tile, more):
                for h in range(2):
                    for c in range(CHUNKS):
                        high2(chunks, h * CHUNKS + c)
                    if h == 0 or more:
                        exps(tile + (h + 1), 1 - h)
                    act.wait_ge(av_done, chunks + (LEAD + CHUNKS * (h + 1)))
                    act.wait_ge(rin_done, tile + (h + 1))
                    nc.scalar.activation(PEB[:, h, 0:D], PS[:, 7, D:2 * D], ACT.Copy, scale=RIN)\
                      .then_inc(right_done, 1)

            with act.Fori(0, LAYERS) as layer:
                base = layer * PAIRS
                act.wait_ge(av_done, layer * (PAIRS * BODY) + LEAD)
                transposed_high2(base, 0, 0)
                with act.Fori(0, (PAIRS - 1) // 2) as half:
                    p2 = half * 2
                    for j in range(2):
                        transposed_high2(base, p2 + (j + 1), (j + 1) % 2)
                        outputs_high2(base, p2 + j)
                outputs_high2(base, PAIRS - 1)
                exps(layer * T, 0)
                with act.Fori(0, PAIRS - 1) as pr:
                    steps_act(layer * (PAIRS * BODY) + pr * BODY, layer * T + pr * 2, True)
                steps_act(layer * (PAIRS * BODY) + (PAIRS - 1) * BODY, layer * T + (T - 2), False)

        @block.vector
        def _(dve):
            for s in (glo_done, h2lo_done, masked, lo_done, a_copied, wslo_done, wtlo_done, whlo_done,
                      ev_done, m_done, o_read):
                dve.sem_inc(s, LEAD)

            dve.wait_ge(w_in, 32)
            for side in range(2):
                nc.vector.tensor_tensor(PEB[:, :, 0:D] if side == 0 else PAB[:, :, 0:D],
                                        WRAW0[:, :, GX:GX + D],
                                        AROW[:, side * D:(side + 1) * D].unsqueeze(1).broadcast_to([P, K, D]),
                                        ALU.mult).then_inc(wv_step, 1)
            dve.wait_ge(wv_step, 2)
            nc.vector.reduce_sum(WV[:, 0, :], PEB[:, :, 0:D], AX).then_inc(wv_step, 1)
            nc.vector.reduce_sum(WV[:, 1, :], PAB[:, :, 0:D], AX).then_inc(wv_step, 1)
            dve.wait_ge(wv_step, 4)
            nc.vector.tensor_copy(WRAW0[:, :, GX + D + 2:GX + D + 3], WV[:, 1, :].unsqueeze(2)).then_inc(wv_step, 1)
            nc.vector.memset(WRAW0[:, :, GX + D + 3:WC], 0.0).then_inc(wv_step, 1)
            nc.vector.tensor_copy(WSL[:, 0, :, :], WV[:, 0, :].unsqueeze(2).broadcast_to([P, K, P]))\
              .then_inc(wv_step, 1)
            dve.wait_ge(wv_step, 7)
            nc.vector.tensor_copy(WX[:, 0, :, :], WRAW0).then_inc(wv_step, 1)
            nc.vector.tensor_tensor(WSL[:, 1, :, :], WV[:, 0, :].unsqueeze(2).broadcast_to([P, K, P]),
                                    WSL[:, 0, :, :].bitcast(F32), ALU.subtract).then_inc(w_ready, 1)
            dve.wait_ge(wv_step, 8)
            nc.vector.tensor_tensor(WX[:, 1, :, :], WRAW0, WX[:, 0, :, :].bitcast(F32), ALU.subtract)\
              .then_inc(w_ready, 1)

            def statistics(pr, count):
                for h in range(2):
                    last = nc.vector.bn_stats(BN[:, h, :], X[:, bass.ds(2 * pr + h, 1), :].squeeze(1))
                last.then_inc(stat, 1)
                reached = dve.to_reg(count + 1)
                dve.wait_ge(w_ready, 2)
                dve.wait_ge(stat, reached)
                for h in range(2):
                    last = nc.vector.bn_aggr(AG[:, h, :], BN[:, h, :])
                last.then_inc(stat2, 1)
                dve.wait_ge(stat2, count + 1)
                nc.vector.tensor_copy(MV[:, bass.ds(2 * pr, 2), :], AG).then_inc(stat3, 1)
                reached = dve.to_reg(count + 1)
                dve.wait_ge(w_ready, 2)
                dve.wait_ge(stat3, reached)

            def scales(n):
                v, sq, r, t = (LNT[:, i, :] for i in range(4))
                step = n * 6
                nc.vector.tensor_scalar(v, MV[:, :, 1], EPS_LN, None, ALU.add).then_inc(ln_in, 1)
                dve.wait_ge(ln_sqrt, n + 1)
                nc.vector.reciprocal(r, sq).then_inc(ln_step, 1)
                dve.wait_ge(ln_step, step + 1)
                nc.vector.tensor_tensor(t, v, r, ALU.mult).then_inc(ln_step, 1)
                dve.wait_ge(ln_step, step + 2)
                nc.vector.tensor_tensor(t, t, sq, ALU.add).then_inc(ln_step, 1)
                dve.wait_ge(ln_step, step + 3)
                nc.vector.tensor_scalar(t, t, 0.5, None, ALU.mult).then_inc(ln_step, 1)
                dve.wait_ge(ln_step, step + 4)
                nc.vector.reciprocal(RSTD, t).then_inc(ln_step, 1)
                dve.wait_ge(ln_step, step + 5)
                nc.vector.tensor_tensor(NMR, MV[:, :, 0], RSTD, ALU.mult).then_inc(ln_step, 1)
                dve.wait_ge(ln_step, step + 6)
                nc.vector.tensor_scalar(NMR, NMR, -1.0, None, ALU.mult).then_inc(ln_done, 1)

            dve.wait_ge(x_in[0], 16)
            with dve.Fori(0, 7) as pr:
                statistics(pr, pr)
            dve.wait_ge(x_in[1], 16)
            with dve.Fori(7, PAIRS) as pr:
                statistics(pr, pr)
            scales(0)

            def transposed_low(pr, b):
                dve.wait_ge(hthi_done, pr + 1)
                nc.vector.tensor_tensor(HT[b][:, 1, :, :], PS[:, 4, :].rearrange("p (k n) -> p k n", k=K),
                                        HT[b][:, 0, :, :].bitcast(F32), ALU.subtract).then_inc(htlo_done, 1)

            def outputs_low(pr):
                for h in range(2):
                    g = G[:, bass.ds(2 * pr + h, 1), :].squeeze(1)
                    dve.wait_ge(ghi_done, pr * 2 + (h + 1))
                    nc.vector.tensor_tensor(g[:, GX:2 * GX], PS[:, h, 0:GX], g[:, 0:GX].bitcast(F32),
                                            ALU.subtract).then_inc(glo_done, 1)
                for h in range(2):
                    ra = RA[:, bass.ds(2 * pr + h, 1), :].squeeze(1)
                    dve.wait_ge(h2hi_done, pr * 2 + (h + 1))
                    nc.vector.tensor_copy(XA[:, bass.ds(2 * pr + h, 1), :].squeeze(1), PS[:, 2 + h, D:D + 2])
                    nc.vector.tensor_copy(SR[:, bass.ds(2 * pr + h, 1)], PS[:, 2 + h, D + 2:D + 3])
                    nc.vector.tensor_tensor(ra[:, GX:GX + D], PS[:, 2 + h, 0:D], ra[:, 0:D].bitcast(F32),
                                            ALU.subtract).then_inc(h2lo_done, 1)

            transposed_low(0, 0)
            with dve.Fori(0, (PAIRS - 1) // 2) as half:
                p2 = half * 2
                for j in range(2):
                    transposed_low(p2 + (j + 1), (j + 1) % 2)
                    outputs_low(p2 + j)
            outputs_low(PAIRS - 1)

            def leaky1(pr, u):
                s = AF[:, WORK1[u % UNITS], :]
                dve.wait_ge(s_done, pr * UNITS + (u + 1))
                nc.vector.scalar_tensor_tensor(s, s, SLOPE, s, ALU.mult, ALU.max).then_inc(lr_done, 1)

            def mask1(pr, u):
                q, i = u // UNITS, u % UNITS
                s = AF[:, WORK1[i], :]
                dve.wait_ge(e_done, pr * UNITS + (u + 1))
                dve.wait_ge(stage_full[STAGE[i]], staged(pr + q, i))
                nc.vector.tensor_tensor(s, s, STG[:, STAGE[i], :], ALU.mult).then_inc(masked, 1)

            def low1(pr, u):
                dve.wait_ge(hi_done, pr * UNITS + (u + 1))
                nc.vector.tensor_tensor(FR[:, AL + HALF1[u], :], AF[:, WORK1[u], :],
                                        FR[:, AH + HALF1[u], :].bitcast(F32), ALU.subtract).then_inc(lo_done, 1)

            def post_bias(pr):
                for h in range(2):
                    if h == 0:
                        dve.wait_ge(first_done, pr + 1)
                    else:
                        dve.wait_ge(mm_done, pr * UNITS + (LEAD + UNITS))
                    nc.vector.tensor_tensor(PAB[:, h, :], PS[:, 2 + h, 0:GX], BIAS[:, :], ALU.add)\
                      .then_inc(a_copied, 1)
                dve.wait_ge(a_copied, pr * 2 + (LEAD + 2))
                dve.wait_ge(e_copied, pr * 2 + (LEAD + 2))
                nc.vector.tensor_tensor(ZZ, PAB[:, :, D:GX], XA[:, bass.ds(2 * pr, 2), :], ALU.add)\
                  .then_inc(z_ready, 1)
                nc.vector.tensor_scalar(DN, PEB[:, :, D], EPS_DEN, None, ALU.add).then_inc(post1, 1)

            def post_mix(pr):
                dve.wait_ge(post1, pr * 6 + 1)
                nc.vector.reciprocal(DN, DN).then_inc(post1, 1)
                dve.wait_ge(sg_ready, pr + 1)
                nc.vector.tensor_scalar(SG, SG, 0.5, 0.5, ALU.mult, ALU.add).then_inc(post1, 1)
                dve.wait_ge(post1, pr * 6 + 3)
                nc.vector.tensor_tensor(CA, SG[:, :, 0], DN, ALU.mult).then_inc(post1, 1)
                for h in range(2):
                    last = nc.vector.tensor_scalar(PAB[:, h, 0:D], PAB[:, h, 0:D], SG[:, h, 1:2], None, ALU.mult)
                last.then_inc(post1, 1)
                dve.wait_ge(post1, pr * 6 + 5)
                for h in range(2):
                    last = nc.vector.scalar_tensor_tensor(PEB[:, h, 0:D], PEB[:, h, 0:D], CA[:, h:h + 1],
                                                          PAB[:, h, 0:D], ALU.mult, ALU.add)
                last.then_inc(v_ready, 1)

            def post_x1(pr):
                x = X[:, bass.ds(2 * pr, 2), :]
                dve.wait_ge(th_ready, pr + 1)
                nc.vector.scalar_tensor_tensor(x, PEB[:, :, 0:D], 0.5, x, ALU.mult, ALU.add).then_inc(post1, 1)
                dve.wait_ge(post1, pr * 6 + 6)
                nc.vector.tensor_scalar(x, x, 0.5, None, ALU.add).then_inc(x1_ready, 1)
                reached = dve.to_reg(pr + 1)
                dve.wait_ge(w_ready, 2)
                dve.wait_ge(x1_ready, reached)
                statistics(pr, PAIRS + pr)

            def units_dve(pr, post, more):
                for u in range(UNITS):
                    if u + 2 < UNITS or more:
                        leaky1(pr, u + 2)
                    if u + 1 < UNITS or more:
                        mask1(pr, u + 1)
                    low1(pr, u)
                    if post and u == 0:
                        post_bias(pr - 1)
                    if post and u == 2:
                        post_mix(pr - 1)
                    if post and u == 4:
                        post_x1(pr - 1)

            leaky1(0, 0)
            leaky1(0, 1)
            mask1(0, 0)
            units_dve(0, False, True)
            with dve.Fori(1, PAIRS - 1) as pr:
                units_dve(pr, True, True)
            units_dve(PAIRS - 1, True, False)
            post_bias(PAIRS - 1)
            post_mix(PAIRS - 1)
            post_x1(PAIRS - 1)
            scales(1)

            nc.vector.memset(ROW[:, :, N:NP], 0.0).then_inc(pad_zero, 1)

            def transposed_low2(base, pr, b):
                dve.wait_ge(hthi1_done, base + (pr + 1))
                nc.vector.tensor_tensor(HT[b][:, 1, :, :], PS[:, 7, :].rearrange("p (k n) -> p k n", k=K),
                                        HT[b][:, 0, :, :].bitcast(F32), ALU.subtract).then_inc(htlo1_done, 1)

            def outputs_low2(base, pr):
                dve.wait_ge(wshi_done, base + (pr + 1))
                nc.vector.tensor_tensor(WsT[:, 1, :, bass.ds(pr * 256, 256)],
                                        PS[:, 0, :].rearrange("p (k n) -> p k n", k=K),
                                        WsT[:, 0, :, bass.ds(pr * 256, 256)].bitcast(F32), ALU.subtract)\
                  .then_inc(wslo_done, 1)
                dve.wait_ge(wthi_done, base + (pr + 1))
                for h in range(2):
                    last = nc.vector.tensor_tensor(
                        WHS[:, h, 1, :, :], PS[:, 1, :].rearrange("p (d h n) -> p h d n", d=K, h=2)[:, h, :, :],
                        WHS[:, h, 0, :, :].bitcast(F32), ALU.subtract)
                last.then_inc(wtlo_done, 1)
                dve.wait_ge(whhi_done, base + (pr + 1))
                nc.vector.tensor_tensor(RA[:, bass.ds(2 * pr, 2), D:2 * D],
                                        PS[:, 2, :].rearrange("p (h c) -> p h c", h=2),
                                        RA[:, bass.ds(2 * pr, 2), 0:D].bitcast(F32), ALU.subtract)\
                  .then_inc(whlo_done, 1)

            def evacuate(chunks, tile, c):
                h, k = c // CHUNKS, c % CHUNKS
                if k == 0:
                    dve.wait_ge(t_done, chunks + (LEAD + (h - 1) * CHUNKS))
                dve.wait_ge(sc_done, chunks + (LEAD + c + 1))
                nc.vector.tensor_scalar(ROW[:, h % 2, k * C:k * C + REAL[k]], PS[:, SBANK[c % BODY], 0:REAL[k]],
                                        1.0, None, ALU.mult, ALU.max, accum_out=MX[:, k:k + 1])\
                  .then_inc(ev_done, 1)

            def maximum(chunks, tile, h):
                dve.wait_ge(ev_done, chunks + (LEAD + (h + 1) * CHUNKS))
                nc.vector.reduce_max(NMX[:, h % 2:h % 2 + 1], MX, AX, negate=True).then_inc(max_done, 1)
                reached = dve.to_reg(tile + (h + 1))
                dve.wait_ge(w_ready, 2)
                dve.wait_ge(max_done, reached)

            def mask2(chunks, tile, c):
                h, k = c // CHUNKS, c % CHUNKS
                w = WIDTH[k]
                dve.wait_ge(t_done, chunks + (LEAD + c + 1))
                if h == 0 and k * (C // P) in (PART_J[0][0], PART_J[1][0]):
                    dve.wait_ge(adj8_full[int(k > 0)], (tile + 2) * 8)
                dve.wait_ge(alo_done, chunks + (LEAD + before(WORK2, c) + 1))
                j0, j1 = k * (C // P), k * (C // P) + w // P
                nc.vector.tensor_tensor(AF[:, WORK2[c], 0:w].rearrange("p (j i) -> p j i", i=P),
                                        PS[:, 5 + TBANK[c], 0:w].rearrange("p (j i) -> p j i", i=P),
                                        A8[:, j0:j1, h * P:(h + 1) * P], ALU.mult).then_inc(m_done, 1)

            def post2(tile, h, x):
                dve.wait_ge(right_done, tile + (h + 1))
                nc.vector.scalar_tensor_tensor(PAB[:, h, 0:D], PS[:, 7, 0:D], RIN, PEB[:, h, 0:D],
                                               ALU.mult, ALU.add).then_inc(o_read, 1)
                dve.wait_ge(o_read, tile + (h + 1) + LEAD)
                nc.vector.tensor_tensor(PAB[:, h, 0:D], PAB[:, h, 0:D], x, ALU.add).then_inc(res_done, 1)
                dve.wait_ge(res_done, tile + (h + 1))
                nc.vector.scalar_tensor_tensor(x, PAB[:, h, 0:D], SLOPE, PAB[:, h, 0:D], ALU.mult, ALU.max)\
                  .then_inc(x_ready, 1)

            def row_sum(chunks, tile, h):
                dve.wait_ge(p_done, chunks + (h + 1) * CHUNKS)
                nc.vector.reduce_sum(DEN, SM[:, h, 0:CHUNKS], AX).then_inc(sum_step, 1)
                dve.wait_ge(sum_step, tile + (h + 1))
                nc.vector.reciprocal(RIN, DEN).then_inc(rin_done, 1)

            def steps_dve(chunks, tile, pr, more):
                for h in range(2):
                    scores = h == 0 or more
                    nxt = (h + 1) * CHUNKS
                    if scores:
                        evacuate(chunks, tile, nxt)
                        evacuate(chunks, tile, nxt + 1)
                    for k in range(CHUNKS):
                        mask2(chunks, tile, h * CHUNKS + k)
                        if scores and k + 2 < CHUNKS:
                            evacuate(chunks, tile, nxt + k + 2)
                        if scores and k + 2 == CHUNKS:
                            maximum(chunks, tile, h + 1)
                    row_sum(chunks, tile, h)
                    post2(tile, h, X[:, bass.ds(2 * pr + h, 1), :].squeeze(1))

            with dve.Fori(0, LAYERS) as layer:
                base = layer * PAIRS
                dve.wait_ge(w1_in, layer * 16 + 16)
                nc.vector.tensor_copy(WX[:, 0, :, 0:2 * D], WRAW1).then_inc(w1_hi, 1)
                dve.wait_ge(w1_hi, layer + 1)
                nc.vector.tensor_tensor(WX[:, 1, :, 0:2 * D], WRAW1, WX[:, 0, :, 0:2 * D].bitcast(F32),
                                        ALU.subtract).then_inc(w1_ready, 1)
                transposed_low2(base, 0, 0)
                with dve.Fori(0, (PAIRS - 1) // 2) as half:
                    p2 = half * 2
                    for j in range(2):
                        transposed_low2(base, p2 + (j + 1), (j + 1) % 2)
                        outputs_low2(base, p2 + j)
                outputs_low2(base, PAIRS - 1)
                chunks0, tile0 = layer * (PAIRS * BODY), layer * T
                for k in range(CHUNKS):
                    evacuate(chunks0, tile0, k)
                maximum(chunks0, tile0, 0)
                with dve.Fori(0, PAIRS - 1) as pr:
                    steps_dve(chunks0 + pr * BODY, tile0 + pr * 2, pr, True)
                steps_dve(chunks0 + (PAIRS - 1) * BODY, tile0 + (T - 2), PAIRS - 1, False)

            back = ROW[:, :, :].rearrange("p h (t d) -> p (h t) d", d=D)
            dve.wait_ge(x_ready, (LAYERS + 1) * T)
            for i, (t0, t1) in enumerate(((0, PAIRS), (PAIRS, T))):
                dve.wait_ge(x1_back[i], 16)
                nc.vector.tensor_tensor(X[:, t0:t1, :], X[:, t0:t1, :], back[:, t0:t1, :], ALU.add)\
                  .then_inc(out_ready, 1)

        @block.tensor
        def _(pe):
            for s in (tp_done, h2_mm, mm_done, tp1_done, wh_mm, sc_done, t_done, av_done):
                pe.sem_inc(s, LEAD)

            def product3(out, stationary, moving, n0=None):
                passes = [(0, 0), (0, 1), (1, 0)]
                for k in range(K):
                    for i, (a, b) in enumerate(passes):
                        last = nc.tensor.matmul(out, stationary(a, k), moving(b, k),
                                                start=(k == 0 and i == 0), stop=(k == K - 1 and i == 2))
                return last

            def transpose_pair(bank):
                for k in range(K):
                    for h in range(2):
                        last = nc.tensor.transpose(PS[:, bank, (2 * k + h) * P:(2 * k + h + 1) * P],
                                                   HN[:, h, k * P:(k + 1) * P], IDN[:, :])
                return last

            def transpose0(pr):
                pe.wait_ge(hn_done, pr + 1)
                transpose_pair(4).then_inc(tp_done, 1)

            def products0(pr, b):
                pe.wait_ge(slb_done, pr + LEAD)
                product3(PS[:, 5, 0:256], lambda a, k: WSL[:, a, k, :], lambda c, k: HT[b][:, c, k, :])\
                    .then_inc(sl_mm, 1)
                for h in range(2):
                    pe.wait_ge(glo_done, pr * 2 + LEAD)
                    product3(PS[:, h, 0:GX], lambda a, k: HT[b][:, a, k, h * P:(h + 1) * P],
                             lambda c, k: WX[:, c, k, 0:GX]).then_inc(g_mm, 1)
                for h in range(2):
                    pe.wait_ge(h2lo_done, pr * 2 + LEAD)
                    product3(PS[:, 2 + h, 0:HX], lambda a, k: HT[b][:, a, k, h * P:(h + 1) * P],
                             lambda c, k: WX[:, c, k, GX:GX + HX]).then_inc(h2_mm, 1)

            pe.wait_ge(ident, 1)
            pe.wait_ge(w_ready, 2)
            transpose0(0)
            with pe.Fori(0, (PAIRS - 1) // 2) as half:
                p2 = half * 2
                for j in range(2):
                    pe.wait_ge(htlo_done, p2 + (j + 1))
                    transpose0(p2 + (j + 1))
                    products0(p2 + j, j)
            pe.wait_ge(htlo_done, PAIRS)
            products0(PAIRS - 1, (PAIRS - 1) % 2)

            pe.wait_ge(glo_done, T + LEAD)
            pe.wait_ge(h2lo_done, T + LEAD)
            pe.wait_ge(ones_set, 2)
            with pe.Fori(0, PAIRS) as pr:
                for u in range(UNITS):
                    s = HALF1[u]
                    pe.wait_ge(adjr_done, pr * UNITS + (LEAD + u + 1))
                    pe.wait_ge(lo_done, pr * UNITS + (LEAD + u + 1))
                    for h in range(2):
                        if u == 0:
                            pe.wait_ge(e_copied, pr * 2 + (LEAD + h - 1))
                            pe.wait_ge(a_copied, pr * 2 + (LEAD + h - 1))
                        for jj in range(2):
                            j = 2 * u + jj
                            first, final = j == 0, j == T - 1
                            i0 = (2 * jj + h) * P
                            e_hi, e_lo, adj = (FR[:, r + s, i0:i0 + P] for r in (AH, AL, RR))
                            nc.tensor.matmul(PS[:, h, 0:GX], e_hi, RA[:, j, 0:GX], start=first, stop=False)
                            nc.tensor.matmul(PS[:, h, 0:D], e_hi, RA[:, j, GX:GX + D], start=False, stop=False)
                            nc.tensor.matmul(PS[:, h, 0:GX], e_lo, RA[:, j, 0:GX], start=False, stop=final)
                            nc.tensor.matmul(PS[:, 2 + h, 0:GX], adj, G[:, j, 0:GX], start=first, stop=False)
                            last = nc.tensor.matmul(PS[:, 2 + h, 0:GX], adj, G[:, j, GX:2 * GX],
                                                    start=False, stop=final)
                        if h == 1:
                            last.then_inc(mm_done, 1)
                        elif u == UNITS - 1:
                            last.then_inc(first_done, 1)

            def transpose2(base, pr):
                pe.wait_ge(hn1_done, base + (pr + 1))
                transpose_pair(7).then_inc(tp1_done, 1)

            def products2(base, pr, b):
                pe.wait_ge(wslo_done, base + pr + LEAD)
                for d in range(K):
                    last = product3(PS[:, 0, d * 256:(d + 1) * 256],
                                    lambda a, k: WX[:, a, k, D + d * P:D + (d + 1) * P],
                                    lambda c, k: HT[b][:, c, k, :])
                last.then_inc(ws_mm, 1)
                pe.wait_ge(wtlo_done, base + pr + LEAD)
                for d in range(K):
                    last = product3(PS[:, 1, d * 256:(d + 1) * 256],
                                    lambda a, k: WX[:, a, k, d * P:(d + 1) * P],
                                    lambda c, k: HT[b][:, c, k, :])
                last.then_inc(wt_mm, 1)
                pe.wait_ge(whlo_done, base + pr + LEAD)
                for h in range(2):
                    last = product3(PS[:, 2, h * D:(h + 1) * D],
                                    lambda a, k: HT[b][:, a, k, h * P:(h + 1) * P],
                                    lambda c, k: WX[:, c, k, 0:D])
                last.then_inc(wh_mm, 1)

            def scores(chunks, tile, c):
                h, k = c // CHUNKS % 2, c % CHUNKS
                if k == 0:
                    pe.wait_ge(whT_full[h], (tile + (c // CHUNKS - h) + 2) * 8)
                pe.wait_ge(ev_done, chunks + (LEAD + c - c % BODY + before(SBANK, c % BODY) + 1))
                wht = FR[:, RR + h, :].rearrange("p (s d n) -> p s d n", s=2, d=K)
                product3(PS[:, SBANK[c % BODY], 0:WIDTH[k]], lambda a, d: wht[:, a, d, :],
                         lambda b, d: WsT[:, b, d, k * C:k * C + WIDTH[k]]).then_inc(sc_done, 1)

            def transposes(chunks, c):
                h, k = c // CHUNKS, c % CHUNKS
                pe.wait_ge(p_done, chunks + (c + 1))
                pe.wait_ge(m_done, chunks + (LEAD + before(TBANK, c) + 1))
                for b in range(WIDTH[k] // P):
                    last = nc.tensor.transpose(PS[:, 5 + TBANK[c], b * P:(b + 1) * P],
                                               ROW[:, h, k * C + b * P:k * C + (b + 1) * P], IDN[:, :])
                last.then_inc(t_done, 1)

            def weigh(chunks, tile, c):
                h, k = c // CHUNKS, c % CHUNKS
                pe.wait_ge(alo_done, chunks + (LEAD + c + 1))
                if k == 0:
                    pe.wait_ge(o_read, tile + h + LEAD)
                blocks = WIDTH[k] // P
                for b in range(blocks):
                    j = k * (C // P) + b
                    hi, lo = (FR[:, r + HALF2[c], b * P:(b + 1) * P] for r in (AH, AL))
                    nc.tensor.matmul(PS[:, 7, :], hi, RA[:, j, 0:2 * D], start=(j == 0), stop=False)
                    last = nc.tensor.matmul(PS[:, 7, 0:D], lo, RA[:, j, 0:D], start=False, stop=(j == T - 1))
                last.then_inc(av_done, 1)

            def steps_pe(chunks, tile, more):
                for h in range(2):
                    lead = h == 0 or more
                    cur, nxt = h * CHUNKS, (h + 1) * CHUNKS
                    for k in range(CHUNKS + 2):
                        if lead and k == 0:
                            scores(chunks, tile, nxt)
                        if lead and k + 1 < CHUNKS:
                            scores(chunks, tile, nxt + k + 1)
                        if k < CHUNKS:
                            transposes(chunks, cur + k)
                        if k >= 2:
                            weigh(chunks, tile, cur + k - 2)

            pe.wait_ge(pad_zero, 1)
            with pe.Fori(0, LAYERS) as layer:
                base = layer * PAIRS
                pe.wait_ge(w1_ready, layer + 1)
                pe.wait_ge(o_read, layer * T + LEAD)
                transpose2(base, 0)
                with pe.Fori(0, (PAIRS - 1) // 2) as half:
                    p2 = half * 2
                    for j in range(2):
                        pe.wait_ge(htlo1_done, base + (p2 + (j + 1)))
                        transpose2(base, p2 + (j + 1))
                        products2(base, p2 + j, j)
                pe.wait_ge(htlo1_done, base + PAIRS)
                products2(base, PAIRS - 1, (PAIRS - 1) % 2)

                pe.wait_ge(wslo_done, base + PAIRS + LEAD)
                pe.wait_ge(wtlo_done, base + PAIRS + LEAD)
                pe.wait_ge(whlo_done, base + PAIRS + LEAD)
                chunks0, tile0 = layer * (PAIRS * BODY), layer * T
                for k in range(CHUNKS):
                    scores(chunks0, tile0, k)
                with pe.Fori(0, PAIRS - 1) as pr:
                    steps_pe(chunks0 + pr * BODY, tile0 + pr * 2, True)
                steps_pe(chunks0 + (PAIRS - 1) * BODY, tile0 + (T - 2), False)


def kernel(x, adj, L0_gnn_W_sa, L0_gnn_a_sa, L0_gnn_W_gcnb, L0_gnn_b_gcnb, L0_gnn_Wa, L0_gnn_ba,
           L0_gnn_Wb, L0_gnn_bb, L1_gnn_W_stack):
    import numpy as np
    import concourse.bacc as bacc
    from concourse.bass_utils import run_bass_kernel_spmd

    x, adj = np.asarray(x), np.asarray(adj)
    xt = np.zeros((NP, D), x.dtype)
    xt[:N] = x
    xt = np.ascontiguousarray(xt.reshape(T, P, D).transpose(1, 0, 2))
    adjt = np.zeros((NP, NP), adj.dtype)
    adjt[:N, :N] = adj
    adjt = np.ascontiguousarray(adjt.reshape(PAIRS, 2 * P, T, P).transpose(0, 3, 2, 1))
    wa, wb = np.asarray(L0_gnn_Wa), np.asarray(L0_gnn_Wb)
    wx = np.concatenate([np.asarray(L0_gnn_W_gcnb), wa[:, :D].T, wb[:, :D].T, np.asarray(L0_gnn_W_sa),
                         wa[:, D:].T, wb[:, D:].T], axis=1)
    wx = np.ascontiguousarray(wx.reshape(K, P, -1).transpose(1, 0, 2))
    rows = np.concatenate([np.asarray(L0_gnn_a_sa)[0], np.asarray(L0_gnn_b_gcnb), np.asarray(L0_gnn_ba),
                           np.asarray(L0_gnn_bb)])
    rows = np.ascontiguousarray(np.broadcast_to(rows, (P, rows.size)))
    wst = np.ascontiguousarray(np.asarray(L1_gnn_W_stack).reshape(LAYERS, K, P, 2 * D).transpose(0, 2, 1, 3))

    nc = bacc.Bacc("TRN2", target_bir_lowering=False, num_devices=1)
    arrays = {"xt": xt, "adjt": adjt, "wx": wx, "rows": rows, "wst": wst}
    args = [nc.dram_tensor(n, a.shape, mybir.dt.from_np(a.dtype), kind="ExternalInput").ap()
            for n, a in arrays.items()]
    out = nc.dram_tensor("out", (N, D), F32, kind="ExternalOutput").ap()
    two_graph_blocks(nc, *args, out)
    r = run_bass_kernel_spmd(nc, [arrays], core_ids=[0])
    return r.results[0]["out"]
```

```python
from contextlib import ExitStack

import concourse.bass as bass
from concourse import mybir

F32 = mybir.dt.float32
F32R = mybir.dt.float32r
U8 = mybir.dt.uint8
ALU = mybir.AluOpType
ACT = mybir.ActivationFunctionType
AX = mybir.AxisListType.X

P = 128
N = 3327
T = (N + P - 1) // P
NP = T * P
D = 256
K = D // P
PAIRS = T // 2
LAYERS = 2
SLOPE = 0.01
EPS_LN = 1e-5
EPS_DEN = 1e-5

GX = D + 2
HX = D + 4
WC = GX + HX + 2

X_PARTS = [(0, 8), (8, 16), (16, 22), (22, T)]

UNITS = T // 2
PART_J = [(0, 16), (16, T)]
C = 512
CHUNKS = (N + C - 1) // C
WIDTH = [C] * (CHUNKS - 1) + [NP - C * (CHUNKS - 1)]
REAL = [C] * (CHUNKS - 1) + [N - C * (CHUNKS - 1)]
BODY = 2 * CHUNKS
WHT_STORES = ((PAIRS + 1) // 2, PAIRS // 2)

BACK = [(0, 7), (7, PAIRS), (PAIRS, PAIRS + 7), (PAIRS + 7, T)]

LEAD = 14


def ring(slots, last=()):
    def build(steps):
        whole = (steps - len(last)) if last else steps
        return [i % slots for i in range(whole)] + list(last)
    return build


def before(slots, i):
    n = len(slots)
    j = i - 1
    while slots[j % n] != slots[i]:
        j -= 1
    return j


STAGE = ring(6, [3])(UNITS)
WORK1 = ring(5)(UNITS)
HALF1 = ring(3, [1])(UNITS)
SBANK = ring(5)(BODY)
TBANK = ring(2)(BODY)
WORK2 = ring(5)(BODY)
HALF2 = ring(3)(BODY)
ORDER = "S0 W5 T0 S1 W6 T1 S2 S3 T2 W0 S4 T3 W1 S5 T4 W2 S6 T5 W3 T6 W4".split()
EVACUATE = {0: (1,), 1: (2, 3), 2: (4,), 3: (5,), 4: (6,)}


def two_graph_blocks(nc, xt, adjt, wx, rows, wst, out):
    ctx = ExitStack()
    with ctx:
        def sb(name, shape, dt):
            return ctx.enter_context(nc.sbuf_tensor(name, shape, dt))

        def sem(name):
            return ctx.enter_context(nc.semaphore(name))

        adj8_d = nc.dram_tensor("adj8_scratch", [PAIRS, P, T, 2 * P], U8).ap()
        whT_d = nc.dram_tensor("whT_scratch", [T, P, 2 * K * P], F32).ap()
        x1_d = nc.dram_tensor("x1_scratch", [T, P, D], F32).ap()

        X = sb("X", [P, T, D], F32)
        RA = sb("RA", [P, T, 516], F32R)
        RB = sb("RB", [P, T * 516], F32R)
        G = RB[:, :].rearrange("p (t c) -> p t c", t=T)
        WsT = RB[:, 0:2 * K * NP].rearrange("p (s k n) -> p s k n", s=2, k=K)
        ROW = sb("ROW", [P, 2, NP], F32)
        SLB = ROW[:, 0, :]
        STG = ROW[:, 1, 0:6 * C].rearrange("p (s c) -> p s c", s=6)
        WRAW0 = ROW[:, 1, 0:2 * WC].rearrange("p (k c) -> p k c", k=K)
        AROW = ROW[:, 1, 2 * WC:2 * WC + 2 * D]
        WRAW1 = ROW[:, 0, 0:K * 2 * D].rearrange("p (k c) -> p k c", k=K)
        AF = sb("AF", [P, 5, C], F32)
        HN = AF[:, 4, :].rearrange("p (h c) -> p h c", h=2)
        FR = sb("FR", [P, 9, C], F32R)
        AH, AL, RR = 0, 3, 6
        HT = [FR[:, 2 * b:2 * b + 2, :].rearrange("p s (k n) -> p s k n", k=K) for b in range(2)]
        WHS = [FR[:, 4 + 2 * b:6 + 2 * b, :].rearrange("p h (s d n) -> p h s d n", s=2, d=K) for b in range(2)]
        WSL = FR[:, 8, :].rearrange("p (s k c) -> p s k c", s=2, k=K)
        A8 = sb("A8", [P, T, 2 * P], U8)
        WX = sb("WX", [P, 2, K, WC], F32R)
        PEB = sb("PEB", [P, 2, GX], F32)
        PAB = sb("PAB", [P, 2, GX], F32)
        BIAS = sb("BIAS", [P, GX], F32)
        IDN = sb("IDN", [P, P], F32)
        MV = sb("MV", [P, T, 2], F32)
        BN = sb("BN", [P, 2, 6], F32)
        LNT = sb("LNT", [P, 6, T], F32)
        RSTD, NMR = LNT[:, 4, :], LNT[:, 5, :]
        XA = sb("XA", [P, T, 2], F32)
        SR = sb("SR", [P, T], F32)
        COL = sb("COL", [P, 48], F32)
        WV = COL[:, 0:4].rearrange("p (s k) -> p s k", s=2)
        ZZ = COL[:, 4:8].rearrange("p (h c) -> p h c", h=2)
        SG = COL[:, 8:12].rearrange("p (h c) -> p h c", h=2)
        DN = COL[:, 12:14]
        CA = COL[:, 14:16]
        MX = COL[:, 16:16 + CHUNKS]
        SM = COL[:, 24:40].rearrange("p (h c) -> p h c", h=2)
        NMX = COL[:, 40:42]
        DEN = COL[:, 42:43]
        RIN = COL[:, 43:44]
        AG = COL[:, 44:48].rearrange("p (h c) -> p h c", h=2)
        PS = ctx.enter_context(nc.psum_tensor("PS", [P, 8, C], F32))

        x_in = [sem(f"x_in{i}") for i in range(len(X_PARTS))]
        w_in = sem("w_in")
        const_in = sem("const_in")
        ident0 = sem("ident0")
        ident = sem("ident")
        stat0 = sem("stat0")
        stat = sem("stat")
        stat2 = sem("stat2")
        stat3 = sem("stat3")
        wv_step = sem("wv_step")
        w_ready = sem("w_ready")
        ln_in = sem("ln_in")
        ln_sqrt = sem("ln_sqrt")
        ln_step = sem("ln_step")
        ln_done = sem("ln_done")
        ones_set = sem("ones_set")

        hn_done = sem("hn_done")
        tp_done = sem("tp_done")
        hthi_done = sem("hthi_done")
        htlo_done = sem("htlo_done")
        sl_mm = sem("sl_mm")
        g_mm = sem("g_mm")
        h2_mm = sem("h2_mm")
        slb_done = sem("slb_done")
        ghi_done = sem("ghi_done")
        glo_done = sem("glo_done")
        h2hi_done = sem("h2hi_done")
        h2lo_done = sem("h2lo_done")

        stage_full = [sem(f"stage_full{i}") for i in range(6)]
        s_done = sem("s_done")
        bytes_out = [sem(f"bytes_out{i}") for i in range(6)]
        lr_done = sem("lr_done")
        e_done = sem("e_done")
        masked = sem("masked")
        adjr_done = sem("adjr_done")
        hi_done = sem("hi_done")
        lo_done = sem("lo_done")
        mm_done = sem("mm_done")
        first_done = sem("first_done")
        e_copied = sem("e_copied")
        a_copied = sem("a_copied")
        post1 = sem("post1")
        z_ready = sem("z_ready")
        sg_tanh = sem("sg_tanh")
        sg_ready = sem("sg_ready")
        gated = sem("gated")
        v_tanh = sem("v_tanh")
        v_ready = sem("v_ready")
        th_ready = sem("th_ready")
        x1_ready = sem("x1_ready")
        x1_stored = sem("x1_stored")

        x_ready = sem("x_ready")
        w1_in = sem("w1_in")
        w1_hi = sem("w1_hi")
        w1_ready = sem("w1_ready")
        hn1_done = sem("hn1_done")
        tp1_done = sem("tp1_done")
        hthi1_done = sem("hthi1_done")
        htlo1_done = sem("htlo1_done")
        ws_mm = sem("ws_mm")
        wt_mm = sem("wt_mm")
        wh_mm = sem("wh_mm")
        wshi_done = sem("wshi_done")
        wslo_done = sem("wslo_done")
        wthi_done = sem("wthi_done")
        wtlo_done = sem("wtlo_done")
        whhi_done = sem("whhi_done")
        whlo_done = sem("whlo_done")
        whT_stored = [sem(f"whT_stored{b}") for b in range(2)]

        whT_full = [sem(f"whT_full{i}") for i in range(2)]
        adj8_full = [sem(f"adj8_full{i}") for i in range(2)]
        pad_zero = sem("pad_zero")
        sc_done = sem("sc_done")
        ev_done = sem("ev_done")
        max_done = sem("max_done")
        p_done = sem("p_done")
        t_done = sem("t_done")
        m_done = sem("m_done")
        ahi_done = sem("ahi_done")
        alo_done = sem("alo_done")
        av_done = sem("av_done")
        sum_step = sem("sum_step")
        rin_done = sem("rin_done")
        right_done = sem("right_done")
        o_read = sem("o_read")
        res_done = sem("res_done")

        x1_back = [sem(f"x1_back{i}") for i in range(len(BACK))]
        early_out = sem("early_out")
        late_out = sem("late_out")
        out_stored = sem("out_stored")

        block = ctx.enter_context(nc.Block())

        stage_uses = [STAGE.count(s) for s in range(6)]

        def staged(pr, u):
            return pr * (16 * stage_uses[STAGE[u]]) + 16 * (STAGE[:u].count(STAGE[u]) + 1)


        @block.sync
        def _(sp):
            for b in range(2):
                sp.sem_inc(whT_stored[b], 16)
            sp.dma_start(BIAS[:, :], rows[:, 2 * D:2 * D + GX]).then_inc(const_in, 16)
            sp.dma_start(AROW, rows[:, 0:2 * D]).then_inc(w_in, 16)
            sp.dma_start(WRAW0[:, :, 0:GX + D + 2], wx).then_inc(w_in, 16)
            for i, (t0, t1) in enumerate(X_PARTS):
                sp.dma_start(X[:, t0:t1, :], xt[:, t0:t1, :]).then_inc(x_in[i], 16)

            sp.wait_ge(w_ready, 2)
            def load_unit(pr, u, first):
                b, n = before(STAGE, u), STAGE[:u].count(STAGE[u])
                if not (first and n == 0):
                    read = sp.to_reg(pr * UNITS + (LEAD + b + 1))
                    stored = sp.to_reg(pr * (16 * stage_uses[STAGE[u]]) + 16 * n)
                    sp.wait_ge(w_ready, 2)
                    sp.wait_ge(adjr_done, read)
                    sp.wait_ge(masked, read)
                    sp.wait_ge(bytes_out[STAGE[u]], stored)
                sp.dma_start(STG[:, STAGE[u], :],
                             adjt[bass.ds(pr, 1), :, 2 * u:2 * u + 2, :].rearrange("o p j i -> p (o j i)"))\
                    .then_inc(stage_full[STAGE[u]], 16)

            for u in range(UNITS):
                load_unit(0, u, True)
            with sp.Fori(1, PAIRS) as pr:
                for u in range(UNITS):
                    load_unit(pr, u, False)

            sp.wait_ge(s_done, PAIRS * UNITS)
            for i in range(6):
                sp.wait_ge(bytes_out[i], 16 * PAIRS * stage_uses[i])
            def store_whT(layer, pr, b):
                reached = sp.to_reg(layer * PAIRS + pr + (1 + LEAD))
                sp.wait_ge(w_ready, 2)
                sp.wait_ge(wtlo_done, reached)
                sp.dma_start(whT_d[bass.ds(2 * pr, 2), :, :].rearrange("t p f -> p t f"),
                             FR[:, 4 + 2 * b:6 + 2 * b, :].bitcast(F32)).then_inc(whT_stored[b], 16)

            with sp.Fori(0, LAYERS) as layer:
                reached = sp.to_reg(layer * (PAIRS * BODY) + (LEAD - CHUNKS))
                sp.wait_ge(w_ready, 2)
                sp.wait_ge(t_done, reached)
                sp.dma_start(WRAW1, wst[bass.ds(layer, 1), :, :, :].rearrange("o p k c -> p (o k) c"))\
                  .then_inc(w1_in, 16)
                with sp.Fori(0, (PAIRS - 1) // 2) as half:
                    for j in range(2):
                        store_whT(layer, half * 2 + j, j)
                store_whT(layer, PAIRS - 1, 0)
                for b in range(2):
                    reached = sp.to_reg(layer * (16 * WHT_STORES[b]) + (16 * WHT_STORES[b] + 16))
                    sp.wait_ge(w_ready, 2)
                    sp.wait_ge(whT_stored[b], reached)
                with sp.Fori(0, PAIRS) as pr:
                    for h in range(2):
                        reached = sp.to_reg(layer * (PAIRS * BODY) + pr * BODY + (LEAD + CHUNKS * (h - 1)))
                        sp.wait_ge(w_ready, 2)
                        sp.wait_ge(sc_done, reached)
                        sp.dma_start(FR[:, RR + h, :].bitcast(F32),
                                     whT_d[bass.ds(2 * pr + h, 1), :, :].rearrange("o p f -> p (o f)"))\
                          .then_inc(whT_full[h], 16)
                    for g, (j0, j1) in enumerate(PART_J):
                        reached = sp.to_reg(layer * (PAIRS * BODY) + pr * BODY
                                            + (LEAD - CHUNKS + (j1 * P + C - 1) // C))
                        sp.wait_ge(w_ready, 2)
                        sp.wait_ge(m_done, reached)
                        sp.dma_start(A8[:, j0:j1, :],
                                     adj8_d[bass.ds(pr, 1), :, j0:j1, :].rearrange("o p j i -> p (o j) i"))\
                          .then_inc(adj8_full[g], 16)

            back = ROW[:, :, :].rearrange("p h (t d) -> p (h t) d", d=D)
            for i, (t0, t1) in enumerate(BACK):
                chunks = -(-t1 * D // C) if t1 <= PAIRS else CHUNKS + -(-(t1 - PAIRS) * D // C)
                sp.wait_ge(t_done, LEAD + LAYERS * PAIRS * BODY - BODY + chunks)
                sp.dma_start(back[:, t0:t1, :], x1_d[t0:t1, :, :].rearrange("t p d -> p t d"))\
                  .then_inc(x1_back[i], 16)
            full = T - 1
            for i, (t0, t1) in enumerate(BACK):
                t1 = min(t1, full)
                sp.wait_ge((early_out, late_out)[i // 2], i % 2 + 1)
                sp.dma_start(out[t0 * P:t1 * P, :].rearrange("(t p) d -> p t d", p=P), X[:, t0:t1, :])\
                  .then_inc(out_stored, 16)
            sp.dma_start(out[full * P:N, :], X[0:N - full * P, full, :]).then_inc(out_stored, 16)
            sp.wait_ge(out_stored, 16 * len(BACK) + 16)
            sp.wait_ge(x1_stored, 16 * PAIRS)

        @block.gpsimd
        def _(pool):
            pool.sem_inc(alo_done, LEAD)
            nc.gpsimd.memset(IDN[:, :], 0.0).then_inc(ident0, 1)
            nc.gpsimd.memset(RA[:, :, D:D + 1].bitcast(F32), 1.0).then_inc(ones_set, 1)
            nc.gpsimd.memset(RA[:, :, D + 1:D + 2].bitcast(F32), 0.0).then_inc(ones_set, 1)
            pool.wait_ge(ident0, 1)
            nc.gpsimd.affine_select(out=IDN[:, :], in_=IDN[:, :], compare_op=ALU.not_equal, fill=1.0,
                                    base=0, pattern=[[-1, P]], channel_multiplier=1).then_inc(ident, 1)

            with pool.Fori(0, PAIRS) as pr:
                for u in range(UNITS):
                    s = WORK1[u]
                    reached = pool.to_reg(pr * UNITS + (LEAD + before(WORK1, u) + 1))
                    left = pool.to_reg(pr + (1 + LEAD))
                    pool.wait_ge(ident, 1)
                    if u == 0:
                        pool.wait_ge(slb_done, left)
                    if u == 4:
                        pool.wait_ge(tp_done, PAIRS + LEAD)
                    pool.wait_ge(h2lo_done, 2 * u + (2 + LEAD))
                    pool.wait_ge(lo_done, reached)
                    nc.gpsimd.tensor_tensor(
                        AF[:, s, :].rearrange("p (j i) -> p j i", j=2),
                        SLB[:, bass.ds(pr * 256, 256)].unsqueeze(1).broadcast_to([P, 2, 256]),
                        SR[:, 2 * u:2 * u + 2].unsqueeze(2).broadcast_to([P, 2, 256]),
                        ALU.add).then_inc(s_done, 1)
                    landed = pool.to_reg(staged(pr, u))
                    pool.wait_ge(ident, 1)
                    pool.wait_ge(stage_full[STAGE[u]], landed)
                    pool.wait_ge(ident, 1)
                    pool.dma_start(adj8_d[bass.ds(pr, 1), :, 2 * u:2 * u + 2, :].rearrange("o p j i -> p (o j i)"),
                                   STG[:, STAGE[u], :]).then_inc(bytes_out[STAGE[u]], 16)

            pool.wait_ge(lo_done, PAIRS * UNITS + LEAD)
            with pool.Fori(0, LAYERS) as layer:
                with pool.Fori(0, PAIRS) as pr:
                    pool.wait_ge(x_ready, layer * T + pr * 2 + 2)
                    pool.wait_ge(tp1_done, layer * PAIRS + pr + LEAD)
                    reached = pool.to_reg(layer * (PAIRS * BODY) + LEAD)
                    pool.wait_ge(ident, 1)
                    pool.wait_ge(av_done, reached)
                    nc.gpsimd.tensor_copy(HN, X[:, bass.ds(2 * pr, 2), :]).then_inc(hn1_done, 1)
                with pool.Fori(0, PAIRS) as pr:
                    for c in range(BODY):
                        w = WIDTH[c % CHUNKS]
                        pool.wait_ge(ahi_done, layer * (PAIRS * BODY) + pr * BODY + (c + 1))
                        nc.gpsimd.tensor_tensor(FR[:, AL + HALF2[c], 0:w], AF[:, WORK2[c], 0:w],
                                                FR[:, AH + HALF2[c], 0:w].bitcast(F32), ALU.subtract)\
                          .then_inc(alo_done, 1)

            back = ROW[:, :, :].rearrange("p h (t d) -> p (h t) d", d=D)
            for i, (t0, t1) in enumerate(BACK[:2]):
                pool.wait_ge(x_ready, LAYERS * T + t1)
                pool.wait_ge(x1_back[i], 16)
                nc.gpsimd.tensor_tensor(X[:, t0:t1, :], X[:, t0:t1, :], back[:, t0:t1, :], ALU.add)\
                  .then_inc(early_out, 1)

        @block.scalar
        def _(act):
            for s in (slb_done, adjr_done, e_copied):
                act.sem_inc(s, LEAD)

            act.wait_ge(ln_in, 1)
            nc.scalar.activation(LNT[:, 1, :], LNT[:, 0, :], ACT.Sqrt).then_inc(ln_sqrt, 1)

            def normalise(pr):
                act.wait_ge(tp_done, pr + LEAD)
                for h in range(2):
                    last = nc.scalar.activation(HN[:, h, :], X[:, bass.ds(2 * pr + h, 1), :].squeeze(1),
                                                ACT.Relu, scale=RSTD[:, bass.ds(2 * pr + h, 1)],
                                                bias=NMR[:, bass.ds(2 * pr + h, 1)])
                last.then_inc(hn_done, 1)

            def transposed_high(pr, b, peeled=0):
                act.wait_ge(tp_done, pr + 1 + LEAD)
                if peeled or not isinstance(pr, int):
                    act.wait_ge(h2_mm, pr * 2 - 2 + LEAD)
                nc.scalar.activation(HT[b][:, 0, :, :], PS[:, 4, :].rearrange("p (k n) -> p k n", k=K),
                                     ACT.Copy).then_inc(hthi_done, 1)

            def outputs_high(pr):
                act.wait_ge(sl_mm, pr + 1)
                nc.scalar.activation(SLB[:, bass.ds(pr * 256, 256)], PS[:, 5, 0:256], ACT.Copy)\
                  .then_inc(slb_done, 1)
                for h in range(2):
                    act.wait_ge(g_mm, pr * 2 + (h + 1))
                    nc.scalar.activation(G[:, bass.ds(2 * pr + h, 1), 0:GX].squeeze(1),
                                         PS[:, h, 0:GX], ACT.Copy).then_inc(ghi_done, 1)
                for h in range(2):
                    act.wait_ge(h2_mm, pr * 2 + (h + 1) + LEAD)
                    nc.scalar.activation(RA[:, bass.ds(2 * pr + h, 1), 0:D].squeeze(1),
                                         PS[:, 2 + h, 0:D], ACT.Copy).then_inc(h2hi_done, 1)

            act.wait_ge(ln_done, 1)
            normalise(0)
            transposed_high(0, 0)
            normalise(1)
            with act.Fori(0, (PAIRS - 3) // 2) as half:
                p2 = half * 2
                for j in range(2):
                    transposed_high(p2 + (j + 1), (j + 1) % 2)
                    normalise(p2 + (j + 2))
                    outputs_high(p2 + j)
            transposed_high(PAIRS - 2, 1, 2)
            normalise(PAIRS - 1)
            outputs_high(PAIRS - 3)
            transposed_high(PAIRS - 1, 0, 2)
            outputs_high(PAIRS - 2)

            def exp1(pr, u):
                q, i = u // UNITS, u % UNITS
                s = AF[:, WORK1[i], :]
                act.wait_ge(lr_done, pr * UNITS + (u + 1))
                nc.scalar.activation(s, s, ACT.Exp, scale=-1.0).then_inc(e_done, 1)

            def high1(pr, u):
                q, i = u // UNITS, u % UNITS
                free = LEAD + q * UNITS + before(HALF1, i) + 1
                act.wait_ge(mm_done, pr * UNITS + free)
                act.wait_ge(stage_full[STAGE[i]], staged(pr + q, i))
                nc.scalar.activation(FR[:, RR + HALF1[i], :], STG[:, STAGE[i], :], ACT.Copy)\
                  .then_inc(adjr_done, 1)
                act.wait_ge(masked, pr * UNITS + (LEAD + u + 1))
                nc.scalar.activation(FR[:, AH + HALF1[i], :], AF[:, WORK1[i], :], ACT.Copy).then_inc(hi_done, 1)

            def post_copy(pr):
                for h in range(2):
                    if h == 0:
                        act.wait_ge(first_done, pr + 1)
                    else:
                        act.wait_ge(mm_done, pr * UNITS + (LEAD + UNITS))
                    nc.scalar.activation(PEB[:, h, :], PS[:, h, 0:GX], ACT.Copy).then_inc(e_copied, 1)

            def post_gates(pr):
                act.wait_ge(z_ready, pr + 1)
                nc.scalar.activation(SG, ZZ, ACT.Tanh, scale=0.5).then_inc(sg_tanh, 1)
                act.wait_ge(sg_tanh, pr + 1)
                nc.scalar.activation(SG, SG, ACT.Copy, scale=0.5, bias=0.5).then_inc(sg_ready, 1)

            def post_gated(pr):
                act.wait_ge(sg_ready, pr + 1)
                for h in range(2):
                    last = nc.scalar.activation(PAB[:, h, 0:D], PAB[:, h, 0:D], ACT.Copy, scale=SG[:, h, 1:2])
                last.then_inc(gated, 1)

            def post_sigmoid(pr):
                act.wait_ge(v_ready, pr + 1)
                nc.scalar.activation(PEB[:, :, 0:D], PEB[:, :, 0:D], ACT.Tanh, scale=0.5).then_inc(v_tanh, 1)

            def post_sigmoid2(pr):
                act.wait_ge(v_tanh, pr + 1)
                nc.scalar.activation(PEB[:, :, 0:D], PEB[:, :, 0:D], ACT.Copy, scale=0.5, bias=0.5)\
                  .then_inc(th_ready, 1)

            def post_store(pr):
                act.wait_ge(x1_ready, pr + 1)
                act.dma_start(x1_d[bass.ds(2 * pr, 2), :, :].rearrange("t p d -> p t d"),
                              X[:, bass.ds(2 * pr, 2), :]).then_inc(x1_stored, 16)

            def roots(n, t0, t1):
                act.wait_ge(ln_in, n + 1)
                nc.scalar.activation(LNT[:, 1, t0:t1], LNT[:, 0, t0:t1], ACT.Sqrt).then_inc(ln_sqrt, 1)

            def normalise2(pr):
                for t in (2 * pr, 2 * pr + 1):
                    nc.scalar.activation(X[:, t, :], X[:, t, :], ACT.Relu, scale=RSTD[:, t:t + 1],
                                         bias=NMR[:, t:t + 1]).then_inc(x_ready, 1)

            def units_act(pr, post, more, final=False):
                for u in range(UNITS):
                    if u + 2 < UNITS or more:
                        exp1(pr, u + 2)
                    if post and u == 0:
                        post_copy(pr - 1)
                    if u + 1 < UNITS or more:
                        high1(pr, u + 1)
                    if post and u == 1:
                        post_gates(pr - 1)
                    if post and u == 2:
                        post_gated(pr - 1)
                    if post and u == 4:
                        post_sigmoid(pr - 1)
                    if post and u == 5:
                        post_sigmoid2(pr - 1)
                    if post and u == 7:
                        post_store(pr - 1)
                    if final and u == 7:
                        roots(1, 0, T - 2)
                    if final and u == 9:
                        act.wait_ge(ln_done, 2)
                        act.wait_ge(x1_stored, 16 * (PAIRS - 1))
                    if final and u >= 9:
                        normalise2(u - 9)

            exp1(0, 0)
            exp1(0, 1)
            outputs_high(PAIRS - 1)
            high1(0, 0)
            units_act(0, False, True)
            with act.Fori(1, PAIRS - 1) as pr:
                units_act(pr, True, True)
            units_act(PAIRS - 1, True, False, True)
            post_copy(PAIRS - 1)
            normalise2(4)
            normalise2(5)
            post_gates(PAIRS - 1)
            post_gated(PAIRS - 1)
            normalise2(6)
            normalise2(7)
            post_sigmoid(PAIRS - 1)
            normalise2(8)
            post_sigmoid2(PAIRS - 1)
            for pr in range(9, PAIRS - 1):
                normalise2(pr)
            post_store(PAIRS - 1)
            roots(2, T - 2, T)
            act.wait_ge(ln_done, 3)
            act.wait_ge(x1_stored, 16 * PAIRS)
            normalise2(PAIRS - 1)

            def transposed_high2(base, pr, b):
                act.wait_ge(tp1_done, base + (pr + 1) + LEAD)
                if not isinstance(pr, int):
                    act.wait_ge(wh_mm, base + (pr - 1) + LEAD)
                nc.scalar.activation(HT[b][:, 0, :, :], PS[:, 7, :].rearrange("p (k n) -> p k n", k=K),
                                     ACT.Copy).then_inc(hthi1_done, 1)

            def outputs_high2(base, layer, pr, b):
                act.wait_ge(ws_mm, base + (pr + 1))
                nc.scalar.activation(WsT[:, 0, :, bass.ds(pr * 256, 256)],
                                     PS[:, 0, :].rearrange("p (k n) -> p k n", k=K), ACT.Copy)\
                  .then_inc(wshi_done, 1)
                act.wait_ge(wt_mm, base + (pr + 1))
                act.wait_ge(whT_stored[b], layer * (16 * WHT_STORES[b]) + (pr - b) * 8 + 16)
                nc.scalar.activation(WHS[b][:, :, 0, :, :],
                                     PS[:, 1, :].rearrange("p (d h n) -> p h d n", d=K, h=2), ACT.Copy)\
                  .then_inc(wthi_done, 1)
                act.wait_ge(wh_mm, base + (pr + 1) + LEAD)
                nc.scalar.activation(RA[:, bass.ds(2 * pr, 2), 0:D],
                                     PS[:, 2, :].rearrange("p (h c) -> p h c", h=2), ACT.Copy)\
                  .then_inc(whhi_done, 1)

            def exps(tile, h, parts):
                if parts[0] == 0:
                    act.wait_ge(max_done, tile + 1)
                for c in parts:
                    r = ROW[:, h, c * C:c * C + REAL[c]]
                    nc.scalar.activation(r, r, ACT.Exp, bias=NMX[:, h:h + 1], accum_out=SM[:, h, c:c + 1])\
                      .then_inc(p_done, 1)

            def high2(chunks, c):
                w, s = WIDTH[c % CHUNKS], HALF2[c]
                act.wait_ge(m_done, chunks + (LEAD + c + 1))
                act.wait_ge(av_done, chunks + (LEAD + before(HALF2, c) + 1))
                nc.scalar.activation(FR[:, AH + s, 0:w], AF[:, WORK2[c], 0:w], ACT.Copy).then_inc(ahi_done, 1)

            def right_part(chunks, tile, h):
                act.wait_ge(av_done, chunks + (LEAD + CHUNKS * (h + 1)))
                act.wait_ge(rin_done, tile + (h + 1))
                nc.scalar.activation(PEB[:, h % 2, 0:D], PS[:, 7, D:2 * D], ACT.Copy, scale=RIN)\
                  .then_inc(right_done, 1)

            def steps_act(chunks, tile, first, last):
                for h in range(2):
                    for k in range(CHUNKS):
                        high2(chunks, h * CHUNKS + k)
                        if k == 0 and not (first and h == 0):
                            right_part(chunks, tile, h - 1)
                        if k >= CHUNKS - 3 and not (last and h == 1):
                            exps(tile + (h + 1), 1 - h, ((0, 1), (2, 3), (4, 5, 6))[k - (CHUNKS - 3)])

            with act.Fori(0, LAYERS) as layer:
                base = layer * PAIRS
                act.wait_ge(av_done, layer * (PAIRS * BODY) + LEAD)
                transposed_high2(base, 0, 0)
                with act.Fori(0, (PAIRS - 1) // 2) as half:
                    p2 = half * 2
                    for j in range(2):
                        transposed_high2(base, p2 + (j + 1), (j + 1) % 2)
                        outputs_high2(base, layer, p2 + j, j)
                outputs_high2(base, layer, PAIRS - 1, 0)
                chunks0, tile0 = layer * (PAIRS * BODY), layer * T
                exps(tile0, 0, range(CHUNKS))
                steps_act(chunks0, tile0, True, False)
                with act.Fori(1, PAIRS - 1) as pr:
                    steps_act(chunks0 + pr * BODY, tile0 + pr * 2, False, False)
                steps_act(chunks0 + (PAIRS - 1) * BODY, tile0 + (T - 2), False, True)
                right_part(chunks0 + (PAIRS - 1) * BODY, tile0 + (T - 2), 1)

        @block.vector
        def _(dve):
            for s in (glo_done, h2lo_done, masked, lo_done, a_copied, wslo_done, wtlo_done, whlo_done,
                      ev_done, m_done, o_read):
                dve.sem_inc(s, LEAD)

            dve.wait_ge(w_in, 32)
            for side in range(2):
                nc.vector.tensor_tensor(PEB[:, :, 0:D] if side == 0 else PAB[:, :, 0:D],
                                        WRAW0[:, :, GX:GX + D],
                                        AROW[:, side * D:(side + 1) * D].unsqueeze(1).broadcast_to([P, K, D]),
                                        ALU.mult).then_inc(wv_step, 1)
            dve.wait_ge(wv_step, 2)
            nc.vector.reduce_sum(WV[:, 0, :], PEB[:, :, 0:D], AX).then_inc(wv_step, 1)
            nc.vector.reduce_sum(WV[:, 1, :], PAB[:, :, 0:D], AX).then_inc(wv_step, 1)
            dve.wait_ge(wv_step, 4)
            nc.vector.tensor_copy(WRAW0[:, :, GX + D + 2:GX + D + 3], WV[:, 1, :].unsqueeze(2)).then_inc(wv_step, 1)
            nc.vector.memset(WRAW0[:, :, GX + D + 3:WC], 0.0).then_inc(wv_step, 1)
            nc.vector.tensor_copy(WSL[:, 0, :, :], WV[:, 0, :].unsqueeze(2).broadcast_to([P, K, P]))\
              .then_inc(wv_step, 1)
            dve.wait_ge(wv_step, 7)
            nc.vector.tensor_copy(WX[:, 0, :, :], WRAW0).then_inc(wv_step, 1)
            nc.vector.tensor_tensor(WSL[:, 1, :, :], WV[:, 0, :].unsqueeze(2).broadcast_to([P, K, P]),
                                    WSL[:, 0, :, :].bitcast(F32), ALU.subtract).then_inc(w_ready, 1)
            dve.wait_ge(wv_step, 8)
            nc.vector.tensor_tensor(WX[:, 1, :, :], WRAW0, WX[:, 0, :, :].bitcast(F32), ALU.subtract)\
              .then_inc(w_ready, 1)

            def statistics(pr, count):
                for h in range(2):
                    last = nc.vector.bn_stats(BN[:, h, :], X[:, bass.ds(2 * pr + h, 1), :].squeeze(1))
                last.then_inc(stat, 1)
                reached = dve.to_reg(count + 1)
                dve.wait_ge(w_ready, 2)
                dve.wait_ge(stat, reached)
                for h in range(2):
                    last = nc.vector.bn_aggr(AG[:, h, :], BN[:, h, :])
                last.then_inc(stat2, 1)
                dve.wait_ge(stat2, count + 1)
                nc.vector.tensor_copy(MV[:, bass.ds(2 * pr, 2), :], AG).then_inc(stat3, 1)
                reached = dve.to_reg(count + 1)
                dve.wait_ge(w_ready, 2)
                dve.wait_ge(stat3, reached)

            def aggregate(i):
                dve.wait_ge(stat0, min(2 * i + 2, 2 * len(X_PARTS) - 1) if i else 2)
                for t in range(*X_PARTS[i]):
                    last = nc.vector.bn_aggr(MV[:, t, :], bn0[:, t, :])
                last.then_inc(stat0, 1)

            def variances(n, t0, t1):
                nc.vector.tensor_scalar(LNT[:, 0, t0:t1], MV[:, t0:t1, 1], EPS_LN, None, ALU.add)\
                  .then_inc(ln_in, 1)

            def scales(n, t0, t1):
                v, sq, r, t, rstd, nmr = (LNT[:, i, t0:t1] for i in range(6))
                step = n * 6
                dve.wait_ge(ln_sqrt, n + 1)
                nc.vector.reciprocal(r, sq).then_inc(ln_step, 1)
                dve.wait_ge(ln_step, step + 1)
                nc.vector.tensor_tensor(t, v, r, ALU.mult).then_inc(ln_step, 1)
                dve.wait_ge(ln_step, step + 2)
                nc.vector.tensor_tensor(t, t, sq, ALU.add).then_inc(ln_step, 1)
                dve.wait_ge(ln_step, step + 3)
                nc.vector.tensor_scalar(t, t, 0.5, None, ALU.mult).then_inc(ln_step, 1)
                dve.wait_ge(ln_step, step + 4)
                nc.vector.reciprocal(rstd, t).then_inc(ln_step, 1)
                dve.wait_ge(ln_step, step + 5)
                nc.vector.tensor_tensor(nmr, MV[:, t0:t1, 0], rstd, ALU.mult).then_inc(ln_step, 1)
                dve.wait_ge(ln_step, step + 6)
                nc.vector.tensor_scalar(nmr, nmr, -1.0, None, ALU.mult).then_inc(ln_done, 1)

            bn0 = PAB[:, :, :].rearrange("p h c -> p (h c)")[:, 0:6 * T].rearrange("p (t c) -> p t c", t=T)
            for i, (t0, t1) in enumerate(X_PARTS):
                dve.wait_ge(x_in[i], 16)
                for t in range(t0, t1):
                    last = nc.vector.bn_stats(bn0[:, t, :], X[:, t, :])
                last.then_inc(stat0, 1)
                if i > 0:
                    aggregate(i - 1)
            aggregate(len(X_PARTS) - 1)
            dve.wait_ge(stat0, 2 * len(X_PARTS))
            variances(0, 0, T)
            scales(0, 0, T)

            def transposed_low(pr, b):
                dve.wait_ge(hthi_done, pr + 1)
                nc.vector.tensor_tensor(HT[b][:, 1, :, :], PS[:, 4, :].rearrange("p (k n) -> p k n", k=K),
                                        HT[b][:, 0, :, :].bitcast(F32), ALU.subtract).then_inc(htlo_done, 1)

            def outputs_low(pr):
                for h in range(2):
                    g = G[:, bass.ds(2 * pr + h, 1), :].squeeze(1)
                    dve.wait_ge(ghi_done, pr * 2 + (h + 1))
                    nc.vector.tensor_tensor(g[:, GX:2 * GX], PS[:, h, 0:GX], g[:, 0:GX].bitcast(F32),
                                            ALU.subtract).then_inc(glo_done, 1)
                for h in range(2):
                    ra = RA[:, bass.ds(2 * pr + h, 1), :].squeeze(1)
                    dve.wait_ge(h2hi_done, pr * 2 + (h + 1))
                    nc.vector.tensor_copy(XA[:, bass.ds(2 * pr + h, 1), :].squeeze(1), PS[:, 2 + h, D:D + 2])
                    nc.vector.tensor_copy(SR[:, bass.ds(2 * pr + h, 1)], PS[:, 2 + h, D + 2:D + 3])
                    nc.vector.tensor_tensor(ra[:, GX:GX + D], PS[:, 2 + h, 0:D], ra[:, 0:D].bitcast(F32),
                                            ALU.subtract).then_inc(h2lo_done, 1)

            transposed_low(0, 0)
            with dve.Fori(0, (PAIRS - 1) // 2) as half:
                p2 = half * 2
                for j in range(2):
                    transposed_low(p2 + (j + 1), (j + 1) % 2)
                    outputs_low(p2 + j)
            def leaky1(pr, u):
                s = AF[:, WORK1[u % UNITS], :]
                dve.wait_ge(s_done, pr * UNITS + (u + 1))
                nc.vector.scalar_tensor_tensor(s, s, SLOPE, s, ALU.mult, ALU.max).then_inc(lr_done, 1)

            def mask1(pr, u):
                q, i = u // UNITS, u % UNITS
                s = AF[:, WORK1[i], :]
                dve.wait_ge(e_done, pr * UNITS + (u + 1))
                dve.wait_ge(stage_full[STAGE[i]], staged(pr + q, i))
                nc.vector.tensor_tensor(s, s, STG[:, STAGE[i], :], ALU.mult).then_inc(masked, 1)

            def low1(pr, u):
                dve.wait_ge(hi_done, pr * UNITS + (u + 1))
                nc.vector.tensor_tensor(FR[:, AL + HALF1[u], :], AF[:, WORK1[u], :],
                                        FR[:, AH + HALF1[u], :].bitcast(F32), ALU.subtract).then_inc(lo_done, 1)

            def post_bias(pr):
                for h in range(2):
                    if h == 0:
                        dve.wait_ge(first_done, pr + 1)
                    else:
                        dve.wait_ge(mm_done, pr * UNITS + (LEAD + UNITS))
                    nc.vector.tensor_tensor(PAB[:, h, :], PS[:, 2 + h, 0:GX], BIAS[:, :], ALU.add)\
                      .then_inc(a_copied, 1)
                dve.wait_ge(a_copied, pr * 2 + (LEAD + 2))
                dve.wait_ge(e_copied, pr * 2 + (LEAD + 2))
                nc.vector.tensor_tensor(ZZ, PAB[:, :, D:GX], XA[:, bass.ds(2 * pr, 2), :], ALU.add)\
                  .then_inc(z_ready, 1)
                nc.vector.tensor_scalar(DN, PEB[:, :, D], EPS_DEN, None, ALU.add).then_inc(post1, 1)

            def post_mix(pr):
                dve.wait_ge(post1, pr * 3 + 1)
                nc.vector.reciprocal(DN, DN).then_inc(post1, 1)
                dve.wait_ge(post1, pr * 3 + 2)
                dve.wait_ge(sg_ready, pr + 1)
                nc.vector.tensor_tensor(CA, SG[:, :, 0], DN, ALU.mult).then_inc(post1, 1)
                dve.wait_ge(post1, pr * 3 + 3)
                dve.wait_ge(gated, pr + 1)
                for h in range(2):
                    last = nc.vector.scalar_tensor_tensor(PEB[:, h, 0:D], PEB[:, h, 0:D], CA[:, h:h + 1],
                                                          PAB[:, h, 0:D], ALU.mult, ALU.add)
                last.then_inc(v_ready, 1)

            def post_x1(pr):
                x = X[:, bass.ds(2 * pr, 2), :]
                dve.wait_ge(th_ready, pr + 1)
                nc.vector.tensor_tensor(x, PEB[:, :, 0:D], x, ALU.add).then_inc(x1_ready, 1)
                reached = dve.to_reg(pr + 1)
                dve.wait_ge(w_ready, 2)
                dve.wait_ge(x1_ready, reached)
                statistics(pr, pr)

            def units_dve(pr, post, more, final=False):
                for u in range(UNITS):
                    if u + 2 < UNITS or more:
                        leaky1(pr, u + 2)
                    if u + 1 < UNITS or more:
                        mask1(pr, u + 1)
                    low1(pr, u)
                    if post and u == 0:
                        post_bias(pr - 1)
                    if post and u == 3:
                        post_mix(pr - 1)
                    if post and u == 6:
                        post_x1(pr - 1)
                    if final and u == 7:
                        variances(1, 0, T - 2)
                    if final and u == 8:
                        scales(1, 0, T - 2)

            leaky1(0, 0)
            leaky1(0, 1)
            outputs_low(PAIRS - 1)
            mask1(0, 0)
            units_dve(0, False, True)
            with dve.Fori(1, PAIRS - 1) as pr:
                units_dve(pr, True, True)
            units_dve(PAIRS - 1, True, False, True)
            post_bias(PAIRS - 1)
            post_mix(PAIRS - 1)
            post_x1(PAIRS - 1)
            variances(2, T - 2, T)
            scales(2, T - 2, T)

            nc.vector.memset(ROW[:, :, N:NP], 0.0).then_inc(pad_zero, 1)

            def transposed_low2(base, pr, b):
                dve.wait_ge(hthi1_done, base + (pr + 1))
                nc.vector.tensor_tensor(HT[b][:, 1, :, :], PS[:, 7, :].rearrange("p (k n) -> p k n", k=K),
                                        HT[b][:, 0, :, :].bitcast(F32), ALU.subtract).then_inc(htlo1_done, 1)

            def outputs_low2(base, pr, b):
                dve.wait_ge(wshi_done, base + (pr + 1))
                nc.vector.tensor_tensor(WsT[:, 1, :, bass.ds(pr * 256, 256)],
                                        PS[:, 0, :].rearrange("p (k n) -> p k n", k=K),
                                        WsT[:, 0, :, bass.ds(pr * 256, 256)].bitcast(F32), ALU.subtract)\
                  .then_inc(wslo_done, 1)
                dve.wait_ge(wthi_done, base + (pr + 1))
                for h in range(2):
                    last = nc.vector.tensor_tensor(
                        WHS[b][:, h, 1, :, :], PS[:, 1, :].rearrange("p (d h n) -> p h d n", d=K, h=2)[:, h, :, :],
                        WHS[b][:, h, 0, :, :].bitcast(F32), ALU.subtract)
                last.then_inc(wtlo_done, 1)
                dve.wait_ge(whhi_done, base + (pr + 1))
                nc.vector.tensor_tensor(RA[:, bass.ds(2 * pr, 2), D:2 * D],
                                        PS[:, 2, :].rearrange("p (h c) -> p h c", h=2),
                                        RA[:, bass.ds(2 * pr, 2), 0:D].bitcast(F32), ALU.subtract)\
                  .then_inc(whlo_done, 1)

            def evacuate(chunks, tile, c):
                h, k = c // CHUNKS, c % CHUNKS
                if k == 0:
                    dve.wait_ge(t_done, chunks + (LEAD + (h - 1) * CHUNKS))
                dve.wait_ge(sc_done, chunks + (LEAD + c + 1))
                nc.vector.tensor_scalar(ROW[:, h % 2, k * C:k * C + REAL[k]], PS[:, SBANK[c % BODY], 0:REAL[k]],
                                        1.0, None, ALU.mult, ALU.max, accum_out=MX[:, k:k + 1])\
                  .then_inc(ev_done, 1)

            def maximum(chunks, tile, h):
                dve.wait_ge(ev_done, chunks + (LEAD + (h + 1) * CHUNKS))
                nc.vector.reduce_max(NMX[:, h % 2:h % 2 + 1], MX, AX, negate=True).then_inc(max_done, 1)
                reached = dve.to_reg(tile + (h + 1))
                dve.wait_ge(w_ready, 2)
                dve.wait_ge(max_done, reached)

            def mask2(chunks, tile, c):
                h, k = c // CHUNKS, c % CHUNKS
                w = WIDTH[k]
                dve.wait_ge(t_done, chunks + (LEAD + c + 1))
                if h == 0 and k * (C // P) in (PART_J[0][0], PART_J[1][0]):
                    dve.wait_ge(adj8_full[int(k > 0)], (tile + 2) * 8)
                dve.wait_ge(alo_done, chunks + (LEAD + before(WORK2, c) + 1))
                j0, j1 = k * (C // P), k * (C // P) + w // P
                nc.vector.tensor_tensor(AF[:, WORK2[c], 0:w].rearrange("p (j i) -> p j i", i=P),
                                        PS[:, 5 + TBANK[c], 0:w].rearrange("p (j i) -> p j i", i=P),
                                        A8[:, j0:j1, h * P:(h + 1) * P], ALU.mult).then_inc(m_done, 1)

            def row_sum(chunks, tile, h):
                dve.wait_ge(p_done, chunks + (h + 1) * CHUNKS)
                nc.vector.reduce_sum(DEN, SM[:, h % 2, 0:CHUNKS], AX).then_inc(sum_step, 1)
                dve.wait_ge(sum_step, tile + (h + 1))
                nc.vector.reciprocal(RIN, DEN).then_inc(rin_done, 1)

            def sums_out(tile, h):
                dve.wait_ge(right_done, tile + (h + 1))
                nc.vector.scalar_tensor_tensor(PAB[:, h % 2, 0:D], PS[:, 7, 0:D], RIN, PEB[:, h % 2, 0:D],
                                               ALU.mult, ALU.add).then_inc(o_read, 1)

            def residual(tile, h, x):
                dve.wait_ge(o_read, tile + (h + 1) + LEAD)
                nc.vector.tensor_tensor(PAB[:, h % 2, 0:D], PAB[:, h % 2, 0:D], x, ALU.add).then_inc(res_done, 1)
                dve.wait_ge(res_done, tile + (h + 1))
                nc.vector.scalar_tensor_tensor(x, PAB[:, h % 2, 0:D], SLOPE, PAB[:, h % 2, 0:D], ALU.mult, ALU.max)\
                  .then_inc(x_ready, 1)

            def steps_dve(chunks, tile, pr, first, last):
                for h in range(2):
                    scores = not (last and h == 1)
                    post = not (first and h == 0)
                    nxt = (h + 1) * CHUNKS
                    for k in range(CHUNKS):
                        if scores and k == 0:
                            evacuate(chunks, tile, nxt)
                        if post and k == 0:
                            row_sum(chunks, tile, h - 1)
                        mask2(chunks, tile, h * CHUNKS + k)
                        if scores and k in EVACUATE:
                            for n in EVACUATE[k]:
                                evacuate(chunks, tile, nxt + n)
                        if post and k == 0:
                            sums_out(tile, h - 1)
                        if post and k == 1:
                            residual(tile, h - 1, X[:, bass.ds(2 * pr + (h - 1), 1), :].squeeze(1))
                        if scores and k == CHUNKS - 3:
                            maximum(chunks, tile, h + 1)

            with dve.Fori(0, LAYERS) as layer:
                base = layer * PAIRS
                dve.wait_ge(w1_in, layer * 16 + 16)
                nc.vector.tensor_copy(WX[:, 0, :, 0:2 * D], WRAW1).then_inc(w1_hi, 1)
                dve.wait_ge(w1_hi, layer + 1)
                nc.vector.tensor_tensor(WX[:, 1, :, 0:2 * D], WRAW1, WX[:, 0, :, 0:2 * D].bitcast(F32),
                                        ALU.subtract).then_inc(w1_ready, 1)
                transposed_low2(base, 0, 0)
                with dve.Fori(0, (PAIRS - 1) // 2) as half:
                    p2 = half * 2
                    for j in range(2):
                        transposed_low2(base, p2 + (j + 1), (j + 1) % 2)
                        outputs_low2(base, p2 + j, j)
                outputs_low2(base, PAIRS - 1, 0)
                chunks0, tile0 = layer * (PAIRS * BODY), layer * T
                for k in range(CHUNKS):
                    evacuate(chunks0, tile0, k)
                maximum(chunks0, tile0, 0)
                steps_dve(chunks0, tile0, 0, True, False)
                with dve.Fori(1, PAIRS - 1) as pr:
                    steps_dve(chunks0 + pr * BODY, tile0 + pr * 2, pr, False, False)
                steps_dve(chunks0 + (PAIRS - 1) * BODY, tile0 + (T - 2), PAIRS - 1, False, True)
                row_sum(chunks0 + (PAIRS - 1) * BODY, tile0 + (T - 2), 1)
                sums_out(tile0 + (T - 2), 1)
                residual(tile0 + (T - 2), 1, X[:, T - 1, :])

            back = ROW[:, :, :].rearrange("p h (t d) -> p (h t) d", d=D)
            for i, (t0, t1) in enumerate(BACK[2:]):
                dve.wait_ge(x_ready, LAYERS * T + t1)
                dve.wait_ge(x1_back[2 + i], 16)
                nc.vector.tensor_tensor(X[:, t0:t1, :], X[:, t0:t1, :], back[:, t0:t1, :], ALU.add)\
                  .then_inc(late_out, 1)

        @block.tensor
        def _(pe):
            for s in (tp_done, h2_mm, mm_done, tp1_done, wh_mm, sc_done, t_done, av_done):
                pe.sem_inc(s, LEAD)

            def product3(out, stationary, moving, n0=None):
                passes = [(0, 0), (0, 1), (1, 0)]
                for k in range(K):
                    for i, (a, b) in enumerate(passes):
                        last = nc.tensor.matmul(out, stationary(a, k), moving(b, k),
                                                start=(k == 0 and i == 0), stop=(k == K - 1 and i == 2))
                return last

            def transpose_pair(bank):
                for k in range(K):
                    for h in range(2):
                        last = nc.tensor.transpose(PS[:, bank, (2 * k + h) * P:(2 * k + h + 1) * P],
                                                   HN[:, h, k * P:(k + 1) * P], IDN[:, :])
                return last

            def transpose0(pr):
                pe.wait_ge(hn_done, pr + 1)
                transpose_pair(4).then_inc(tp_done, 1)

            def products0(pr, b):
                pe.wait_ge(slb_done, pr + LEAD)
                product3(PS[:, 5, 0:256], lambda a, k: WSL[:, a, k, :], lambda c, k: HT[b][:, c, k, :])\
                    .then_inc(sl_mm, 1)
                for h in range(2):
                    pe.wait_ge(glo_done, pr * 2 + LEAD)
                    product3(PS[:, h, 0:GX], lambda a, k: HT[b][:, a, k, h * P:(h + 1) * P],
                             lambda c, k: WX[:, c, k, 0:GX]).then_inc(g_mm, 1)
                for h in range(2):
                    pe.wait_ge(h2lo_done, pr * 2 + LEAD)
                    product3(PS[:, 2 + h, 0:HX], lambda a, k: HT[b][:, a, k, h * P:(h + 1) * P],
                             lambda c, k: WX[:, c, k, GX:GX + HX]).then_inc(h2_mm, 1)

            pe.wait_ge(ident, 1)
            pe.wait_ge(w_ready, 2)
            transpose0(0)
            with pe.Fori(0, (PAIRS - 1) // 2) as half:
                p2 = half * 2
                for j in range(2):
                    pe.wait_ge(htlo_done, p2 + (j + 1))
                    transpose0(p2 + (j + 1))
                    products0(p2 + j, j)
            pe.wait_ge(htlo_done, PAIRS)
            products0(PAIRS - 1, (PAIRS - 1) % 2)

            pe.wait_ge(glo_done, T + LEAD)
            pe.wait_ge(h2lo_done, T + LEAD)
            pe.wait_ge(ones_set, 2)
            with pe.Fori(0, PAIRS) as pr:
                for u in range(UNITS):
                    s = HALF1[u]
                    pe.wait_ge(adjr_done, pr * UNITS + (LEAD + u + 1))
                    pe.wait_ge(lo_done, pr * UNITS + (LEAD + u + 1))
                    for h in range(2):
                        if u == 0:
                            pe.wait_ge(e_copied, pr * 2 + (LEAD + h - 1))
                            pe.wait_ge(a_copied, pr * 2 + (LEAD + h - 1))
                        for jj in range(2):
                            j = 2 * u + jj
                            first, final = j == 0, j == T - 1
                            i0 = (2 * jj + h) * P
                            e_hi, e_lo, adj = (FR[:, r + s, i0:i0 + P] for r in (AH, AL, RR))
                            nc.tensor.matmul(PS[:, h, 0:GX], e_hi, RA[:, j, 0:GX], start=first, stop=False)
                            nc.tensor.matmul(PS[:, h, 0:D], e_hi, RA[:, j, GX:GX + D], start=False, stop=False)
                            nc.tensor.matmul(PS[:, h, 0:GX], e_lo, RA[:, j, 0:GX], start=False, stop=final)
                            nc.tensor.matmul(PS[:, 2 + h, 0:GX], adj, G[:, j, 0:GX], start=first, stop=False)
                            last = nc.tensor.matmul(PS[:, 2 + h, 0:GX], adj, G[:, j, GX:2 * GX],
                                                    start=False, stop=final)
                        if h == 1:
                            last.then_inc(mm_done, 1)
                        elif u == UNITS - 1:
                            last.then_inc(first_done, 1)

            def transpose2(base, pr):
                pe.wait_ge(hn1_done, base + (pr + 1))
                transpose_pair(7).then_inc(tp1_done, 1)

            def products2(base, pr, b):
                pe.wait_ge(wslo_done, base + pr + LEAD)
                for d in range(K):
                    last = product3(PS[:, 0, d * 256:(d + 1) * 256],
                                    lambda a, k: WX[:, a, k, D + d * P:D + (d + 1) * P],
                                    lambda c, k: HT[b][:, c, k, :])
                last.then_inc(ws_mm, 1)
                pe.wait_ge(wtlo_done, base + pr + LEAD)
                for d in range(K):
                    last = product3(PS[:, 1, d * 256:(d + 1) * 256],
                                    lambda a, k: WX[:, a, k, d * P:(d + 1) * P],
                                    lambda c, k: HT[b][:, c, k, :])
                last.then_inc(wt_mm, 1)
                pe.wait_ge(whlo_done, base + pr + LEAD)
                for h in range(2):
                    last = product3(PS[:, 2, h * D:(h + 1) * D],
                                    lambda a, k: HT[b][:, a, k, h * P:(h + 1) * P],
                                    lambda c, k: WX[:, c, k, 0:D])
                last.then_inc(wh_mm, 1)

            def scores(chunks, tile, c):
                h, k = c // CHUNKS % 2, c % CHUNKS
                if k == 0:
                    pe.wait_ge(whT_full[h], (tile + (c // CHUNKS - h) + 2) * 8)
                pe.wait_ge(ev_done, chunks + (LEAD + c - c % BODY + before(SBANK, c % BODY) + 1))
                wht = FR[:, RR + h, :].rearrange("p (s d n) -> p s d n", s=2, d=K)
                product3(PS[:, SBANK[c % BODY], 0:WIDTH[k]], lambda a, d: wht[:, a, d, :],
                         lambda b, d: WsT[:, b, d, k * C:k * C + WIDTH[k]]).then_inc(sc_done, 1)

            def transposes(chunks, c):
                h, k = c // CHUNKS, c % CHUNKS
                pe.wait_ge(p_done, chunks + (c + 1))
                pe.wait_ge(m_done, chunks + (LEAD + before(TBANK, c) + 1))
                for b in range(WIDTH[k] // P):
                    last = nc.tensor.transpose(PS[:, 5 + TBANK[c], b * P:(b + 1) * P],
                                               ROW[:, h, k * C + b * P:k * C + (b + 1) * P], IDN[:, :])
                last.then_inc(t_done, 1)

            def weigh(chunks, tile, c):
                h, k, i = c // CHUNKS, c % CHUNKS, c % BODY
                pe.wait_ge(alo_done, chunks + (LEAD + c + 1))
                if k == 0:
                    pe.wait_ge(o_read, tile + h + LEAD)
                blocks = WIDTH[k] // P
                for b in range(blocks):
                    j = k * (C // P) + b
                    hi, lo = (FR[:, r + HALF2[i], b * P:(b + 1) * P] for r in (AH, AL))
                    nc.tensor.matmul(PS[:, 7, :], hi, RA[:, j, 0:2 * D], start=(j == 0), stop=False)
                    last = nc.tensor.matmul(PS[:, 7, 0:D], lo, RA[:, j, 0:D], start=False, stop=(j == T - 1))
                last.then_inc(av_done, 1)

            def steps_pe(chunks, tile, first, last):
                for h in range(2):
                    for step in ORDER:
                        kind, k = step[0], int(step[1])
                        if kind == "S" and not (last and h == 1):
                            scores(chunks, tile, (h + 1) * CHUNKS + k)
                        if kind == "T":
                            transposes(chunks, h * CHUNKS + k)
                        if kind == "W" and k < CHUNKS - 2:
                            weigh(chunks, tile, h * CHUNKS + k)
                        if kind == "W" and k >= CHUNKS - 2 and not (first and h == 0):
                            weigh(chunks, tile, (h - 1) * CHUNKS + k)

            pe.wait_ge(pad_zero, 1)
            with pe.Fori(0, LAYERS) as layer:
                base = layer * PAIRS
                pe.wait_ge(w1_ready, layer + 1)
                pe.wait_ge(o_read, layer * T + LEAD)
                transpose2(base, 0)
                with pe.Fori(0, (PAIRS - 1) // 2) as half:
                    p2 = half * 2
                    for j in range(2):
                        pe.wait_ge(htlo1_done, base + (p2 + (j + 1)))
                        transpose2(base, p2 + (j + 1))
                        products2(base, p2 + j, j)
                pe.wait_ge(htlo1_done, base + PAIRS)
                products2(base, PAIRS - 1, (PAIRS - 1) % 2)

                pe.wait_ge(wslo_done, base + PAIRS + LEAD)
                pe.wait_ge(wtlo_done, base + PAIRS + LEAD)
                pe.wait_ge(whlo_done, base + PAIRS + LEAD)
                chunks0, tile0 = layer * (PAIRS * BODY), layer * T
                for k in range(CHUNKS):
                    scores(chunks0, tile0, k)
                steps_pe(chunks0, tile0, True, False)
                with pe.Fori(1, PAIRS - 1) as pr:
                    steps_pe(chunks0 + pr * BODY, tile0 + pr * 2, False, False)
                steps_pe(chunks0 + (PAIRS - 1) * BODY, tile0 + (T - 2), False, True)
                for k in (CHUNKS - 2, CHUNKS - 1):
                    weigh(chunks0 + (PAIRS - 1) * BODY, tile0 + (T - 2), CHUNKS + k)


def kernel(x, adj, L0_gnn_W_sa, L0_gnn_a_sa, L0_gnn_W_gcnb, L0_gnn_b_gcnb, L0_gnn_Wa, L0_gnn_ba,
           L0_gnn_Wb, L0_gnn_bb, L1_gnn_W_stack):
    import numpy as np
    import concourse.bacc as bacc
    from concourse.bass_utils import run_bass_kernel_spmd

    x, adj = np.asarray(x), np.asarray(adj)
    xt = np.zeros((NP, D), x.dtype)
    xt[:N] = x
    xt = np.ascontiguousarray(xt.reshape(T, P, D).transpose(1, 0, 2))
    adjt = np.zeros((NP, NP), adj.dtype)
    adjt[:N, :N] = adj
    adjt = np.ascontiguousarray(adjt.reshape(PAIRS, 2 * P, T, P).transpose(0, 3, 2, 1))
    wa, wb = np.asarray(L0_gnn_Wa), np.asarray(L0_gnn_Wb)
    wx = np.concatenate([np.asarray(L0_gnn_W_gcnb), wa[:, :D].T, wb[:, :D].T, np.asarray(L0_gnn_W_sa),
                         wa[:, D:].T, wb[:, D:].T], axis=1)
    wx = np.ascontiguousarray(wx.reshape(K, P, -1).transpose(1, 0, 2))
    rows = np.concatenate([np.asarray(L0_gnn_a_sa)[0], np.asarray(L0_gnn_b_gcnb), np.asarray(L0_gnn_ba),
                           np.asarray(L0_gnn_bb)])
    rows = np.ascontiguousarray(np.broadcast_to(rows, (P, rows.size)))
    wst = np.ascontiguousarray(np.asarray(L1_gnn_W_stack).reshape(LAYERS, K, P, 2 * D).transpose(0, 2, 1, 3))

    nc = bacc.Bacc("TRN2", target_bir_lowering=False, num_devices=1)
    arrays = {"xt": xt, "adjt": adjt, "wx": wx, "rows": rows, "wst": wst}
    args = [nc.dram_tensor(n, a.shape, mybir.dt.from_np(a.dtype), kind="ExternalInput").ap()
            for n, a in arrays.items()]
    out = nc.dram_tensor("out", (N, D), F32, kind="ExternalOutput").ap()
    two_graph_blocks(nc, *args, out)
    r = run_bass_kernel_spmd(nc, [arrays], core_ids=[0])
    return r.results[0]["out"]
```
